# Optimizing a Trainium2 kernel written in Bass

```python
import numpy as np
import jax
import jax.numpy as jnp

def _softmax(x, axis=-1):
    return jax.nn.softmax(x, axis=axis)

def _gelu(x):
    return jax.nn.gelu(x, approximate=True)

def _silu(x):
    return jax.nn.silu(x)

def _sigmoid(x):
    return jax.nn.sigmoid(x)

def _layernorm(x, axis=-1, eps=1e-05):
    m = jnp.mean(x, axis=axis, keepdims=True)
    v = jnp.var(x, axis=axis, keepdims=True)
    return (x - m) / jnp.sqrt(v + eps)

def _scatter_add(tgt, idx, src, axis=0):
    return tgt.at[idx].add(src)

def _segment_sum(src, seg, n):
    return jax.ops.segment_sum(src, seg, n)
kernel_name = 'mk_seq_preln_d1_jaxref_r8_ed78f1'

def setup_inputs(seed: int=0):
    np.random.seed(seed)
    _w = jnp.asarray

    def _L0_attn_setup():
        import jax, jax.numpy as jnp
        import numpy as np
        N_HEAD = 16
        key = jax.random.key(seed)
        ks = jax.random.split(key, 5)
        B, T, C = (4, 128, 128)
        d = C // N_HEAD
        x = jax.random.normal(ks[0], (B, T, C), dtype=jnp.float32)
        w_attn = jax.random.normal(ks[1], (C, 3 * C), dtype=jnp.float32) * 0.02
        w_proj = jax.random.normal(ks[2], (C, C), dtype=jnp.float32) * 0.02
        embk = 0.02 * jax.random.normal(ks[3], (T, d), dtype=jnp.float32)
        embv = 0.02 * jax.random.normal(ks[4], (T, d), dtype=jnp.float32)
        return {'x': x, 'w_attn': w_attn, 'w_proj': w_proj, 'embk': embk, 'embv': embv}
    _L0_attn_in = _L0_attn_setup()

    def _L0_ffn_setup():
        import jax, jax.numpy as jnp
        import numpy as np
        DIM = 128
        INTER = 128
        N_EXPERTS = 8
        TOPK = 2
        N_SHARED = 2
        key = jax.random.key(seed)
        ks = jax.random.split(key, 10)
        s = 0.02
        return {'x': jax.random.normal(ks[0], (4, 256, DIM), dtype=jnp.float32), 'gate_w': jax.random.normal(ks[1], (N_EXPERTS, DIM), dtype=jnp.float32) * s, 'gate_bias': jax.random.normal(ks[2], (N_EXPERTS,), dtype=jnp.float32) * s, 'w1': jax.random.normal(ks[3], (N_EXPERTS, INTER, DIM), dtype=jnp.float32) * s, 'w3': jax.random.normal(ks[4], (N_EXPERTS, INTER, DIM), dtype=jnp.float32) * s, 'w2': jax.random.normal(ks[5], (N_EXPERTS, DIM, INTER), dtype=jnp.float32) * s, 'sw1': jax.random.normal(ks[6], (N_SHARED * INTER, DIM), dtype=jnp.float32) * s, 'sw3': jax.random.normal(ks[7], (N_SHARED * INTER, DIM), dtype=jnp.float32) * s, 'sw2': jax.random.normal(ks[8], (DIM, N_SHARED * INTER), dtype=jnp.float32) * s}
    _L0_ffn_in = _L0_ffn_setup()
    _d = {'L0_attn_x': _L0_attn_in['x'], 'L0_attn_w_attn': _L0_attn_in['w_attn'], 'L0_attn_w_proj': _L0_attn_in['w_proj'], 'L0_attn_embk': _L0_attn_in['embk'], 'L0_attn_embv': _L0_attn_in['embv'], 'L0_ffn_gate_w': _L0_ffn_in['gate_w'], 'L0_ffn_gate_bias': _L0_ffn_in['gate_bias'], 'L0_ffn_w1': _L0_ffn_in['w1'], 'L0_ffn_w3': _L0_ffn_in['w3'], 'L0_ffn_w2': _L0_ffn_in['w2'], 'L0_ffn_sw1': _L0_ffn_in['sw1'], 'L0_ffn_sw3': _L0_ffn_in['sw3'], 'L0_ffn_sw2': _L0_ffn_in['sw2']}
    _x0 = _d['L0_attn_x']
    _d['L0_attn_x'] = jax.random.normal(jax.random.fold_in(jax.random.key(seed), 1), (8, 512, 128), dtype=_x0.dtype)
    del _x0
    return _d

def reference(L0_attn_x, L0_attn_w_attn, L0_attn_w_proj, L0_attn_embk, L0_attn_embv, L0_ffn_gate_w, L0_ffn_gate_bias, L0_ffn_w1, L0_ffn_w3, L0_ffn_w2, L0_ffn_sw1, L0_ffn_sw3, L0_ffn_sw2):

    def _L0_attn_ref(x, w_attn, w_proj, embk, embv):
        import jax, jax.numpy as jnp
        import numpy as np
        N_HEAD = 16
        B, T, C = x.shape
        H = N_HEAD
        d = C // H
        qkv = x @ w_attn
        q, k, v = jnp.split(qkv, 3, axis=2)
        q = q.reshape(B, T, H, d).transpose(0, 2, 1, 3)
        k = k.reshape(B, T, H, d).transpose(0, 2, 1, 3)
        v = v.reshape(B, T, H, d).transpose(0, 2, 1, 3)
        idx = jnp.arange(T)
        rel = jnp.tril(idx[:, None] - idx[None, :])
        rk = embk[rel]
        rv = embv[rel]
        scale = 1.0 / np.sqrt(d).astype(np.float32)
        att = jnp.einsum('bhtd,bhsd->bhts', q, k) * scale + jnp.einsum('bhtd,tsd->bhts', q, rk)
        causal = idx[None, :] <= idx[:, None]
        att = jnp.where(causal[None, None], att, -jnp.inf)
        att = jax.nn.softmax(att, axis=-1)
        y = jnp.einsum('bhts,bhsd->bhtd', att, v) + jnp.einsum('bhts,tsd->bhtd', att, rv)
        y = y.transpose(0, 2, 1, 3).reshape(B, T, C)
        return y @ w_proj

    def _L0_ffn_ref(x, gate_w, gate_bias, w1, w3, w2, sw1, sw3, sw2):
        import jax, jax.numpy as jnp
        import numpy as np
        DIM = 128
        INTER = 128
        N_EXPERTS = 8
        TOPK = 2
        N_SHARED = 2
        shape = x.shape
        xt = x.reshape(-1, shape[-1])
        scores = jax.nn.softmax((xt @ gate_w.T).astype(jnp.float32), axis=-1)
        _, idx = jax.lax.top_k(scores + gate_bias, TOPK)
        weights = jnp.take_along_axis(scores, idx, axis=1).astype(x.dtype)
        y = jnp.zeros_like(xt)
        for e in range(N_EXPERTS):
            gate_e = jnp.sum(jnp.where(idx == e, weights, 0.0), axis=1)
            h = jax.nn.silu(xt @ w1[e].T) * (xt @ w3[e].T)
            y = y + gate_e[:, None] * (h @ w2[e].T)
        z = jax.nn.silu(xt @ sw1.T) * (xt @ sw3.T) @ sw2.T
        return (y + z).reshape(shape)
    x = L0_attn_x
    x = x + _L0_attn_ref(_layernorm(x, axis=-1), L0_attn_w_attn, L0_attn_w_proj, L0_attn_embk, L0_attn_embv)
    x = x + _L0_ffn_ref(_layernorm(x, axis=-1), L0_ffn_gate_w, L0_ffn_gate_bias, L0_ffn_w1, L0_ffn_w3, L0_ffn_w2, L0_ffn_sw1, L0_ffn_sw3, L0_ffn_sw2)
    return x

_drawn_inputs = setup_inputs


def setup_inputs(seed=0):
    import zlib

    import numpy as np

    out = dict(_drawn_inputs(seed))
    spreads = {}
    factors = {'L0_attn_w_attn': 8.0,
     'L0_attn_w_proj': 8.0,
     'L0_attn_embk': 8.0,
     'L0_attn_embv': 8.0,
     'L0_ffn_gate_w': 8.0,
     'L0_ffn_gate_bias': 8.0,
     'L0_ffn_w1': 8.0,
     'L0_ffn_w3': 8.0,
     'L0_ffn_w2': 8.0,
     'L0_ffn_sw1': 6.881,
     'L0_ffn_sw3': 6.836,
     'L0_ffn_sw2': 6.84}
    for name, (base, spread) in spreads.items():
        noise = np.random.default_rng([zlib.crc32(name.encode()), seed]).standard_normal(out[name].shape)
        drawn = base * np.exp(spread * noise) if base else spread * noise
        out[name] = jnp.asarray(drawn.astype(out[name].dtype))
    for name, factor in factors.items():
        out[name] = (out[name] * factor).astype(out[name].dtype)
    return out
```

```python
from contextlib import ExitStack

import numpy as np

import concourse.bass as bass
from concourse import mybir

F32 = mybir.dt.float32
BF16 = mybir.dt.bfloat16
ALU = mybir.AluOpType
ACT = mybir.ActivationFunctionType
AX = mybir.AxisListType

P = 128
B, T, C = 8, 512, 128
H, D = 16, 8
NI = T // P
NREL = 128
TILES = B * NI
SCALE = 1.0 / np.sqrt(np.float32(D))
EPS = 1e-5
BIG = 1e30

GB = 2
G = B // GB
NH = GB * H
QUADS = NH // 4
Q_PART = [0, 0, 1, 1, 2, 0]
K_PART = [0, 1, 0, 1, 0, 2]
KR = 8 * len(Q_PART)

E = 8
TOPK = 2
NSH = 2
CH = 512


def bank_plan():
    g_uses, t_uses = [], []
    g_uses += [("rel", 0, c) for c in range(8)]
    for i in range(NI):
        for n in range(SLOTS):
            for kind, *what in pe_slot(i, n):
                if kind in ("rel", "rt", "yt", "pj"):
                    g_uses.append((kind, *what))
                if kind in ("tp", "ct"):
                    t_uses.append((kind, *what))
        g_uses += [("rv", i, 0), ("rv", i, 1)]
    g_uses += [("rt", NI - 1), ("yt", NI - 1), ("pj", NI - 1)]
    assert len(g_uses) % 2 == 0 and len(t_uses) % 2 == 0
    bank = {use: n % 2 for uses in (g_uses, t_uses) for n, use in enumerate(uses)}
    before = {use: uses[n - 2] for uses in (g_uses, t_uses) for n, use in enumerate(uses)}
    first = {use for uses in (g_uses, t_uses) for use in uses[:2]}
    return bank, before, first


SLOTS = NH + 9


def pe_slot(i, n):
    ops = []
    if n % 4 == 0 and n // 4 + 1 < QUADS:
        ops.append(("tr", i, n // 4 + 1))
    if n < NH:
        ops.append(("qk", i, n))
    if i and 0 <= n - 3 < NH:
        ops.append(("tp", i, n - 3))
    if i and 0 <= n - 4 < NH:
        ops.append(("av", i, n - 4))
    if n % 4 == 2 and n >= 6 and (n - 6) // 4 < QUADS:
        ops.append(("ct", i, (n - 6) // 4))
    if not i and n % 4 == 0 and n >= 8 and (n - 8) // 4 < QUADS:
        ops += [("av", i, n - 8 + q) for q in range(4)]
    if i + 1 < NI and n % 4 == 1 and n < NH:
        ops.append(("rel", i + 1, n // 4))
    if i and n == 3:
        ops.append(("rt", i - 1))
    if i and n == 7:
        ops.append(("yt", i - 1))
    if i and n == 11:
        ops.append(("pj", i - 1))
    return ops


def wait(engine, signal, n):
    if n > 0:
        engine.wait_ge(signal, n)


def qkv_part(nc, t, x, w_attn, w_proj, e_k, e_k127, e_k127h, e_v, e_v127, part_of_row, q_parts, k_parts, v_dram):
    with ExitStack() as ctx:
        sb = lambda name, shape, dt: ctx.enter_context(nc.sbuf_tensor(name, shape, dt))
        sem = lambda name: ctx.enter_context(nc.semaphore(name))
        ps = lambda name, shape: ctx.enter_context(nc.psum_tensor(name, shape, F32))
        GT = GB * NI
        w_sb = sb("w_attn_sb", [P, 3 * C], F32)
        xg = sb("xg", [P, GT, C], F32)
        xc = sb("xc", [P, GT, C], F32)
        sq = sb("sq", [P, GT, C], F32)
        xn = sb("xn", [P, GT, C], F32)
        stat = sb("stat", [P, 5, GT], F32)
        rstd = sb("rstd", [P, GT], F32)
        xnT = sb("xnT", [P, GT * P], F32)
        parts = sb("parts", [P, 2, 3, GT * P], BF16)
        k32 = sb("k32", [P, GT * P], F32)
        rest = sb("rest", [P, 2, GT * P], F32)
        vg = sb("vg", [P, GT, C], F32)
        ek = sb("ek", [KR, 2 * NREL], F32)
        ekr = sb("ekr", [KR, 2, 2 * NREL], F32)
        ekp = sb("ekp", [KR, 3, 2 * NREL], BF16)
        k127 = sb("k127", [KR, 1], F32)
        k127h = sb("k127h", [P, 1], F32)
        nk127h = sb("nk127h", [P, 1], F32)
        v127 = sb("v127", [P, C], F32)
        rowsel = sb("rowsel", [KR, 3], F32)
        xT_ps = ps("xT_ps", [P, 2, 512])
        q_ps = ps("q_ps", [P, 2, 512])
        k_ps = ps("k_ps", [P, 2, 512])
        v_ps = ps("v_ps", [P, 2, 512])

        masks_done = sem("masks_done")
        const_in = sem("const_in")
        id_done = sem("id_done")
        x_in = sem("x_in")
        xc_done = sem("xc_done")
        sq_done = sem("sq_done")
        var_done = sem("var_done")
        sd_done = sem("sd_done")
        xn_done = sem("xn_done")
        xT_ready = sem("xT_ready")
        xnT_done = sem("xnT_done")
        q_ready = sem("q_ready")
        k_ready = sem("k_ready")
        v_ready = sem("v_ready")
        p1_done = sem("p1_done")
        k32_done = sem("k32_done")
        rest_done = sem("rest_done")
        p2_done = sem("p2_done")
        p3_done = sem("p3_done")
        vg_done = sem("vg_done")
        parts_out = sem("parts_out")
        chain = sem("chain")
        tab = sem("tab")

        x_tiles = x.rearrange("b (i p) c -> p (b i) c", p=P)
        v_tiles = v_dram
        NOUT = 2 * 3 * GB + 1
        NCHAIN = 4
        block = ctx.enter_context(nc.Block())

        @block.sync
        def _(sp):
            for dst, src in ((w_sb, w_attn), (ek, e_k), (k127, e_k127), (k127h, e_k127h), (v127, e_v127),
                             (rowsel, part_of_row)):
                sp.dma_start(dst[:, :], src).then_inc(const_in, 16)
            sp.dma_start(t["tv"][:, :, :], e_v).then_inc(const_in, 16)
            sp.dma_start(t["wp"][:, :], w_proj).then_inc(const_in, 16)
            for g in range(G):
                wait(sp, xc_done, g)
                sp.dma_start(xg[:, :, :], x_tiles[:, bass.ds(g * GT, GT), :]).then_inc(x_in, 16)
                for n, (dst, third) in enumerate(((q_parts, 0), (k_parts, 1))):
                    wait(sp, p3_done, 2 * g + 1 + n)
                    for m in range(3):
                        for b in range(GB):
                            src = parts[:, third, m, b * T:(b + 1) * T]
                            sp.dma_start(dst[m, :, bass.ds(g * GB + b, 1), :, :].rearrange("d a h t -> h d (a t)"),
                                         src).then_inc(parts_out, 16)
                wait(sp, vg_done, g + 1)
                sp.dma_start(v_tiles[:, bass.ds(g * GT, GT), :], vg[:, :, :]).then_inc(parts_out, 16)
            wait(sp, parts_out, 16 * NOUT * G)

        @block.gpsimd
        def _(pool):
            nc.gpsimd.memset(t["ident"][:, :], 0.0).then_inc(id_done, 1)
            wait(pool, id_done, 1)
            nc.gpsimd.affine_select(out=t["ident"][:, :], in_=t["ident"][:, :], compare_op=ALU.not_equal, fill=1.0,
                                    base=0, pattern=[[-1, P]], channel_multiplier=1).then_inc(id_done, 1)
            nc.gpsimd.memset(t["mask_far"][:, :], 1.0).then_inc(masks_done, 1)
            nc.gpsimd.memset(t["mask_big"][:, :], 0.0).then_inc(masks_done, 1)
            wait(pool, masks_done, 2)
            nc.gpsimd.affine_select(out=t["mask_far"][:, :], in_=t["mask_far"][:, :], compare_op=ALU.is_gt, fill=0.0, base=0,
                                    pattern=[[1, P]], channel_multiplier=-1).then_inc(masks_done, 1)
            nc.gpsimd.affine_select(out=t["mask_big"][:, :], in_=t["mask_big"][:, :], compare_op=ALU.is_ge, fill=BIG, base=0,
                                    pattern=[[-1, P]], channel_multiplier=1).then_inc(masks_done, 1)
            for g in range(G):
                for n in range(2):
                    wait(pool, p2_done, 2 * g + 1 + n)
                    nc.gpsimd.tensor_tensor(parts[:, n, 2, :], rest[:, n, :], parts[:, n, 1, :],
                                            ALU.subtract).then_inc(p3_done, 1)

        @block.tensor
        def _(pe):
            wait(pe, id_done, 2)
            wait(pe, const_in, 16 * 8)
            for g in range(G):
                wait(pe, xn_done, g + 1)
                wait(pe, xnT_done, 2 * g)
                for n in range(GT):
                    ins = nc.tensor.transpose(xT_ps[:, n // 4, (n % 4) * P:(n % 4 + 1) * P], xn[:, n, :],
                                              t["ident"][:, :])
                    if n % 4 == 3:
                        ins.then_inc(xT_ready, 1)
                wait(pe, xnT_done, 2 * g + 2)
                wait(pe, rest_done, 2 * g)
                for n in range(2):
                    nc.tensor.matmul(q_ps[:, n, :], w_sb[:, 0:C], xnT[:, n * 512:(n + 1) * 512],
                                     start=True, stop=True).then_inc(q_ready, 1)
                for n in range(2):
                    nc.tensor.matmul(k_ps[:, n, :], w_sb[:, C:2 * C], xnT[:, n * 512:(n + 1) * 512],
                                     start=True, stop=True).then_inc(k_ready, 1)
                wait(pe, vg_done, g)
                for n in range(GT):
                    ins = nc.tensor.matmul(v_ps[:, n // 4, (n % 4) * P:(n % 4 + 1) * P], xnT[:, n * P:(n + 1) * P],
                                           w_sb[:, 2 * C:3 * C], start=True, stop=True)
                ins.then_inc(v_ready, 1)

        @block.scalar
        def _(act):
            wait(act, tab, 2)
            for g in range(G):
                wait(act, xc_done, g + 1)
                nc.scalar.activation(sq[:, :, :], xc[:, :, :], ACT.Square).then_inc(sq_done, 1)
                wait(act, var_done, g + 1)
                nc.scalar.activation(stat[:, 4, :], stat[:, 3, :], ACT.Sqrt).then_inc(sd_done, 1)
                wait(act, v_ready, g)
                for n in range(2):
                    wait(act, xT_ready, 2 * g + 1 + n)
                    nc.scalar.activation(xnT[:, n * 512:(n + 1) * 512], xT_ps[:, n, :], ACT.Copy).then_inc(xnT_done, 1)
                wait(act, parts_out, g * 16 * NOUT)
                wait(act, q_ready, 2 * g + 2)
                nc.scalar.activation(parts[:, 0, 0, :], q_ps[:, :, :], ACT.Copy).then_inc(p1_done, 1)
                wait(act, k_ready, 2 * g + 2)
                nc.scalar.activation(k32[:, :], k_ps[:, :, :], ACT.Identity, bias=nk127h[:, 0:1],
                                     scale=-float(SCALE)).then_inc(k32_done, 1)
                wait(act, k32_done, g + 1)
                nc.scalar.activation(parts[:, 1, 0, :], k32[:, :], ACT.Copy).then_inc(p1_done, 1)
                for n in range(2):
                    wait(act, rest_done, 2 * g + 1 + n)
                    nc.scalar.activation(parts[:, n, 1, :], rest[:, n, :], ACT.Copy).then_inc(p2_done, 1)

        @block.vector
        def _(dve):
            wait(dve, const_in, 16 * 8)
            nc.vector.tensor_scalar(t["tv"][:, :, :], t["tv"][:, :, :], 1.0, None, ALU.mult).then_inc(tab, 1)
            nc.vector.tensor_scalar(nk127h[:, :], k127h[:, :], -1.0, None, ALU.mult).then_inc(tab, 1)
            nc.vector.tensor_scalar(ekr[:, 0, :], ek[:, :], -1.0, k127[:, 0:1], ALU.mult, ALU.add).then_inc(tab, 1)
            wait(dve, tab, 3)
            nc.vector.tensor_tensor(t["tv"][:, :, :], t["tv"][:, :, :],
                                    v127[:, 0:D].unsqueeze(1).to_broadcast([P, NREL, D]), ALU.subtract).then_inc(tab, 1)
            nc.vector.tensor_copy(ekp[:, 0, :], ekr[:, 0, :]).then_inc(tab, 1)
            wait(dve, tab, 5)
            nc.vector.tensor_tensor(ekr[:, 1, :], ekr[:, 0, :], ekp[:, 0, :], ALU.subtract).then_inc(tab, 1)
            wait(dve, tab, 6)
            nc.vector.tensor_copy(ekp[:, 1, :], ekr[:, 1, :]).then_inc(tab, 1)
            wait(dve, tab, 7)
            nc.vector.tensor_tensor(ekp[:, 2, :], ekr[:, 1, :], ekp[:, 1, :], ALU.subtract).then_inc(tab, 1)
            wait(dve, tab, 8)
            nc.vector.tensor_scalar(ekr[:, 0, :], ekp[:, 0, :], rowsel[:, 0:1], None, ALU.mult).then_inc(tab, 1)
            wait(dve, tab, 9)
            nc.vector.scalar_tensor_tensor(out=ekr[:, 1, :], in0=ekp[:, 1, :], scalar=rowsel[:, 1:2],
                                           in1=ekr[:, 0, :], op0=ALU.mult, op1=ALU.add).then_inc(tab, 1)
            wait(dve, tab, 10)
            nc.vector.scalar_tensor_tensor(out=t["te"][:, :], in0=ekp[:, 2, :], scalar=rowsel[:, 2:3],
                                           in1=ekr[:, 1, :], op0=ALU.mult, op1=ALU.add).then_inc(tab, 1)
            for g in range(G):
                wait(dve, x_in, 16 * (g + 1))
                nc.vector.tensor_reduce(stat[:, 0, :], xg[:, :, :], AX.X, ALU.add).then_inc(chain, 1)
                wait(dve, chain, NCHAIN * g + 1)
                nc.vector.tensor_scalar(stat[:, 1, :], stat[:, 0, :], 1.0 / C, None, ALU.mult).then_inc(chain, 1)
                wait(dve, chain, NCHAIN * g + 2)
                nc.vector.tensor_tensor(xc[:, :, :], xg[:, :, :],
                                        stat[:, 1, :].unsqueeze(2).to_broadcast([P, GT, C]),
                                        ALU.subtract).then_inc(xc_done, 1)
                wait(dve, sq_done, g + 1)
                nc.vector.tensor_reduce(stat[:, 2, :], sq[:, :, :], AX.X, ALU.add).then_inc(chain, 1)
                wait(dve, chain, NCHAIN * g + 3)
                nc.vector.tensor_scalar(stat[:, 3, :], stat[:, 2, :], 1.0 / C, EPS, ALU.mult,
                                        ALU.add).then_inc(var_done, 1)
                wait(dve, sd_done, g + 1)
                nc.vector.reciprocal(rstd[:, :], stat[:, 4, :]).then_inc(chain, 1)
                wait(dve, chain, NCHAIN * g + 4)
                wait(dve, xT_ready, 2 * g)
                wait(dve, xc_done, g + 1)
                nc.vector.tensor_tensor(xn[:, :, :], xc[:, :, :],
                                        rstd[:, :].unsqueeze(2).to_broadcast([P, GT, C]),
                                        ALU.mult).then_inc(xn_done, 1)
                wait(dve, p1_done, 2 * g + 1)
                nc.vector.tensor_tensor(rest[:, 0, :], q_ps[:, :, :].rearrange("p a n -> p (a n)"), parts[:, 0, 0, :],
                                        ALU.subtract).then_inc(rest_done, 1)
                wait(dve, p1_done, 2 * g + 2)
                nc.vector.tensor_tensor(rest[:, 1, :], k32[:, :], parts[:, 1, 0, :],
                                        ALU.subtract).then_inc(rest_done, 1)
                wait(dve, v_ready, g + 1)
                wait(dve, parts_out, g * 16 * NOUT)
                nc.vector.tensor_tensor(vg[:, :, :], v_ps[:, :, :].rearrange("p a (n c) -> p (a n) c", c=C),
                                        v127[:, :].unsqueeze(1).to_broadcast([P, GT, C]), ALU.add).then_inc(vg_done, 1)


def attention_part(nc, t, x, q_parts, k_parts, v_dram, x1_dram):
    bank_of, use_before, first_uses = bank_plan()
    with ExitStack() as ctx:
        sb = lambda name, shape, dt: ctx.enter_context(nc.sbuf_tensor(name, shape, dt))
        ps = lambda name, shape: ctx.enter_context(nc.psum_tensor(name, shape, F32))
        signals = []

        def sem(name):
            signals.append(ctx.enter_context(nc.semaphore(name)))
            return signals[-1]

        ident = t["ident"]
        te, tv, wp, mask_far, mask_big = t["te"], t["tv"], t["wp"], t["mask_far"], t["mask_big"]
        kb = sb("kb", [KR, NH, T], BF16)
        qb = sb("qb", [KR, 2, NH, P], BF16)
        vb = sb("vb", [P, GB * NI, C], F32)
        xr = sb("xr", [P, GB * NI, C], F32)
        relS = sb("relS", [P, 2, P, NH], F32)
        rc = sb("rc", [P, 2, 4, P], F32)
        near = sb("near", [P, 2, 4, 2, P], F32)
        nmin = sb("nmin", [P, NI, NH], F32)
        fmin = sb("fmin", [P, NI, NH], F32)
        den = sb("den", [P, NI, NH], F32)
        prob = sb("prob", [P, 3, 4, T], F32)
        ptmp = sb("ptmp", [P, 4, P], F32)
        pc = sb("pc", [P, 2, 4, P], F32)
        pT = sb("pT", [P, 3, T], F32)
        pcT = sb("pcT", [P, 2, NH, P], F32)
        av_sb = sb("av_sb", [P, NH * D], F32)
        rden = sb("rden", [P, NH], F32)
        rsb = sb("rsb", [NH, P, D], F32)
        ysum = sb("ysum", [P, NH, D], F32)
        y = sb("y", [P, NH, D], F32)
        yT = sb("yT", [P, GB * P], F32)
        x1 = sb("x1", [P, 2, GB, C], F32)

        qk_ps = ps("qk_ps", [P, 2, 512])
        tr_ps = ps("tr_ps", [P, 4, P])
        tp_ps = ps("tp_ps", [P, 2, 512])
        g_ps = ps("g_ps", [P, 2, 512])
        av_ps = ps("av_ps", [P, 512])

        k_in = [sem(f"k_in{b}") for b in range(GB)]
        q_in = [sem(f"q_in{n}") for n in range(2)]
        v_in = sem("v_in")
        xr_in = sem("xr_in")
        rel_ready = sem("rel_ready")
        rel_done = sem("rel_done")
        tr_ready = sem("tr_ready")
        rc_done = sem("rc_done")
        near_done = sem("near_done")
        qk_ready = sem("qk_ready")
        far_done = sem("far_done")
        min_done = sem("min_done")
        exp_done = sem("exp_done")
        pc_done = sem("pc_done")
        ptmp_done = sem("ptmp_done")
        tp_ready = sem("tp_ready")
        pT_done = sem("pT_done")
        ct_ready = sem("ct_ready")
        ct_done = sem("ct_done")
        av_done = sem("av_done")
        av_copied = sem("av_copied")
        rv_ready = sem("rv_ready")
        rsb_done = sem("rsb_done")
        rt_ready = sem("rt_ready")
        y_chain = sem("y_chain")
        y_done = sem("y_done")
        yt_ready = sem("yt_ready")
        yt_done = sem("yt_done")
        pj_ready = sem("pj_ready")
        x1_done = sem("x1_done")
        x1_out = [sem(f"x1_out{n}") for n in range(2)]

        READ = {
            "rel": lambda i, c: (rel_done, 8 * i + c + 1),
            "rv": lambda i, half: (rsb_done, 2 * i + half + 1),
            "rt": lambda i: (y_chain, 2 * i + 2),
            "yt": lambda i: (yt_done, i + 1),
            "pj": lambda i: (x1_done, i + 1),
            "tp": lambda i, n: (pT_done, NH * (i - 1) + n + 1),
            "ct": lambda i, u: (ct_done, QUADS * i + u + 1),
        }

        x_tiles = x.rearrange("b (i p) c -> p (b i) c", p=P)
        x1_tiles = x1_dram.rearrange("b (i p) c -> p b i c", p=P)
        cleared = range(min(q.num for q in signals), max(q.num for q in signals) + 1)
        with nc.Fori(0, G) as g:
            with nc.Block() as block:

                @block.sync
                def _(sp):
                    def load_q(g, i):
                        wait(sp, qk_ready, NH * (i - 1))
                        for s, m in enumerate(Q_PART):
                            src = q_parts[m, :, bass.ds(g * GB, GB), :, i * P:(i + 1) * P].rearrange("d b h t -> d (b h) t")
                            sp.dma_start(qb[8 * s:8 * s + 8, i % 2, :, :], src).then_inc(q_in[i % 2], 16)

                    def store(g, i):
                        wait(sp, x1_done, i + 1)
                        sp.dma_start(x1_tiles[:, bass.ds(g * GB, GB), i, :], x1[:, i % 2, :, :]).then_inc(x1_out[i % 2], 16)

                    load_q(g, 0)
                    for b in range(GB):
                        for s, m in enumerate(K_PART):
                            src = k_parts[m, :, bass.ds(g * GB + b, 1), :, :].rearrange("d a h t -> d (a h) t")
                            sp.dma_start(kb[8 * s:8 * s + 8, b * H:(b + 1) * H, :], src).then_inc(k_in[b], 16)
                    load_q(g, 1)
                    sp.dma_start(vb[:, :, :], v_dram[:, bass.ds(g * GB * NI, GB * NI), :]).then_inc(v_in, 16)
                    sp.dma_start(xr[:, :, :], x_tiles[:, bass.ds(g * GB * NI, GB * NI), :]).then_inc(xr_in, 16)
                    load_q(g, 2)
                    store(g, 0)
                    load_q(g, 3)
                    for i in range(1, NI):
                        store(g, i)
                    for n in range(2):
                        sp.wait_ge(x1_out[n], 16 * NI // 2)

                @block.gpsimd
                def _(pool):
                    quad = lambda m: m[:, :].unsqueeze(1).to_broadcast([P, 4, P])

                    def masks(g, i, u):
                        k = QUADS * i + u
                        wait(pool, rc_done, k + 1)
                        wait(pool, min_done, 4 * (k - 1))
                        if i:
                            nc.gpsimd.tensor_tensor(near[:, k % 2, :, 0, :], rc[:, k % 2, :, :], quad(mask_far), ALU.mult)
                        nc.gpsimd.tensor_tensor(near[:, k % 2, :, 1, :], rc[:, k % 2, :, :], quad(mask_big),
                                                ALU.add).then_inc(near_done, 1)

                    def near_probs(g, i, u):
                        k = QUADS * i + u
                        wait(pool, exp_done, 4 * k + 4)
                        wait(pool, pc_done, k - QUADS)
                        nc.gpsimd.tensor_tensor(ptmp[:, :, :], prob[:, k % 3, :, (i - 1) * P:i * P], quad(mask_far),
                                                ALU.mult).then_inc(ptmp_done, 1)
                        wait(pool, ptmp_done, k - QUADS + 1)
                        wait(pool, ct_ready, k - 1)
                        nc.gpsimd.tensor_tensor(pc[:, k % 2, :, :], ptmp[:, :, :], prob[:, k % 3, :, i * P:(i + 1) * P],
                                                ALU.add).then_inc(pc_done, 1)

                    masks(g, 0, 0)
                    for i in range(NI):
                        for n in range(SLOTS):
                            if n % 4 == 2 and (n + 2) // 4 < QUADS:
                                masks(g, i, (n + 2) // 4)
                            if i and n % 4 == 0 and n and n // 4 <= QUADS:
                                near_probs(g, i, n // 4 - 1)
                        if i + 1 < NI:
                            masks(g, i + 1, 0)

                @block.tensor
                def _(pe):
                    def take(g, ring, *use):
                        if use not in first_uses:
                            kind, *what = use_before[use]
                            pe.wait_ge(*READ[kind](*what))
                        return ring[:, bank_of[use], :]

                    def rel(g, i, c):
                        if c == 0:
                            wait(pe, q_in[i % 2], 96 * (i // 2 + 1))
                        bank = take(g, g_ps, "rel", i, c)
                        for a in range(16):
                            tau = 16 * c + a
                            ins = nc.tensor.matmul(bank[:, a * NH:(a + 1) * NH], te[:, P - tau:2 * P - tau],
                                                   qb[:, i % 2, :, tau], start=True, stop=True)
                        ins.then_inc(rel_ready, 1)

                    def tr(g, i, u):
                        k = QUADS * i + u
                        if u == 0:
                            wait(pe, rel_done, 8 * (i + 1))
                        wait(pe, rc_done, k)
                        for q in range(4):
                            ins = nc.tensor.transpose(tr_ps[:, q, :], relS[:, i % 2, :, 4 * u + q], ident[:, :])
                        ins.then_inc(tr_ready, 1)

                    def qk(g, i, n):
                        k = NH * i + n
                        if i == 0 and n % H == 0:
                            wait(pe, k_in[n // H], 96)
                        wait(pe, exp_done, k - 1)
                        nc.tensor.matmul(qk_ps[:, k % 2, 0:(i + 1) * P], qb[:, i % 2, n, :], kb[:, n, 0:(i + 1) * P],
                                         start=True, stop=True).then_inc(qk_ready, 1)

                    def tp(g, i, n):
                        k = NH * i + n
                        bank = take(g, tp_ps, "tp", i, n)
                        wait(pe, exp_done, k + 1)
                        for j in range(i + 1):
                            ins = nc.tensor.transpose(bank[:, j * P:(j + 1) * P],
                                                      prob[:, k // 4 % 3, n % 4, j * P:(j + 1) * P], ident[:, :])
                        ins.then_inc(tp_ready, 1)

                    def av(g, i, n):
                        k = NH * i + n
                        if n == 0:
                            wait(pe, av_copied, i)
                            if i == 0:
                                wait(pe, v_in, 16)
                        if i:
                            wait(pe, pT_done, k - NH + 1)
                        else:
                            wait(pe, ct_done, n // 4 + 1)
                        for j in range(i + 1):
                            lhs = pT[:, (k - NH) % 3, j * P:(j + 1) * P] if i else pcT[:, 0, n, :]
                            ins = nc.tensor.matmul(av_ps[:, n * D:(n + 1) * D], lhs,
                                                   vb[:, n // H * NI + j, (n % H) * D:(n % H + 1) * D],
                                                   start=(j == 0), stop=(j == i))
                        ins.then_inc(av_done, 1)

                    def ct(g, i, u):
                        k = QUADS * i + u
                        bank = take(g, tp_ps, "ct", i, u)
                        if i:
                            wait(pe, pc_done, k - QUADS + 1)
                        else:
                            wait(pe, exp_done, 4 * u + 4)
                        for q in range(4):
                            src = pc[:, k % 2, q, :] if i else prob[:, k % 3, q, 0:P]
                            ins = nc.tensor.transpose(bank[:, q * P:(q + 1) * P], src, ident[:, :])
                        ins.then_inc(ct_ready, 1)

                    def rv(g, i, half):
                        wait(pe, ct_done, QUADS * (i + 1))
                        bank = take(g, g_ps, "rv", i, half)
                        for a in range(64):
                            tau = 64 * half + a
                            ins = nc.tensor.matmul(bank[0:NH, a * D:(a + 1) * D], pcT[:, i % 2, :, tau], tv[:, tau, :],
                                                   start=True, stop=True)
                        ins.then_inc(rv_ready, 1)

                    def rt(g, i):
                        wait(pe, rsb_done, 2 * (i + 1))
                        bank = take(g, g_ps, "rt", i)
                        for d in range(D):
                            ins = nc.tensor.transpose(bank[:, d * NH:(d + 1) * NH], rsb[:, :, d], ident[0:NH, 0:NH])
                        ins.then_inc(rt_ready, 1)

                    def yt(g, i):
                        wait(pe, y_done, i + 1)
                        bank = take(g, g_ps, "yt", i)
                        for b in range(GB):
                            ins = nc.tensor.transpose(bank[:, b * P:(b + 1) * P],
                                                      y[:, b * H:(b + 1) * H, :].rearrange("p h d -> p (h d)"), ident[:, :])
                        ins.then_inc(yt_ready, 1)

                    def pj(g, i):
                        wait(pe, yt_done, i + 1)
                        bank = take(g, g_ps, "pj", i)
                        for b in range(GB):
                            ins = nc.tensor.matmul(bank[:, b * C:(b + 1) * C], yT[:, b * P:(b + 1) * P], wp[:, :],
                                                   start=True, stop=True)
                        ins.then_inc(pj_ready, 1)

                    do = {"rel": rel, "tr": tr, "qk": qk, "tp": tp, "av": av, "ct": ct, "rt": rt, "yt": yt, "pj": pj}
                    for c in range(8):
                        rel(g, 0, c)
                    tr(g, 0, 0)
                    for i in range(NI):
                        for n in range(SLOTS):
                            for kind, *what in pe_slot(i, n):
                                do[kind](g, *what)
                        if i + 1 < NI:
                            tr(g, i + 1, 0)
                        rv(g, i, 0)
                        rv(g, i, 1)
                    rt(g, NI - 1)
                    yt(g, NI - 1)
                    pj(g, NI - 1)

                @block.scalar
                def _(act):
                    def rel_copy(g, i, c):
                        wait(act, rel_ready, 8 * i + c + 1)
                        if c == 0:
                            wait(act, tr_ready, QUADS * (i - 1))
                        nc.scalar.activation(relS[:, i % 2, 16 * c:16 * (c + 1), :],
                                             g_ps[:, bank_of["rel", i, c], :].rearrange("p (t n) -> p t n", n=NH),
                                             ACT.Copy).then_inc(rel_done, 1)

                    def rc_copy(g, i, u):
                        k = QUADS * i + u
                        wait(act, tr_ready, k + 1)
                        wait(act, near_done, k - 1)
                        nc.scalar.activation(rc[:, k % 2, :, :], tr_ps[:, :, :], ACT.Copy).then_inc(rc_done, 1)

                    def exp(g, i, n):
                        k = NH * i + n
                        if n % 4 == 0:
                            u = k // 4 - 3
                            if u >= QUADS:
                                wait(act, pc_done, u - QUADS + 1)
                                wait(act, tp_ready, 4 * (u - QUADS) + 4)
                            else:
                                wait(act, ct_ready, u + 1)
                        wait(act, min_done, k + 1)
                        nc.scalar.activation(prob[:, k // 4 % 3, n % 4, 0:(i + 1) * P], qk_ps[:, k % 2, 0:(i + 1) * P],
                                             ACT.Exp, bias=nmin[:, i, n:n + 1], scale=-1.0,
                                             accum_out=den[:, i, n:n + 1]).then_inc(exp_done, 1)

                    def ct_copy(g, i, u):
                        k = QUADS * i + u
                        bank = bank_of["ct", i, u]
                        wait(act, ct_ready, k + 1)
                        if u == 0:
                            wait(act, rv_ready, 2 * (i - 1))
                            if i == 2:
                                wait(act, av_done, NH)
                        nc.scalar.activation(pcT[:, i % 2, 4 * u:4 * u + 4, :],
                                             tp_ps[:, bank, :].rearrange("p (q t) -> p q t", q=4), ACT.Copy).then_inc(ct_done, 1)

                    def yt_copy(g, i):
                        wait(act, yt_ready, i + 1)
                        wait(act, pj_ready, i)
                        nc.scalar.activation(yT[:, :], g_ps[:, bank_of["yt", i], 0:GB * P], ACT.Copy).then_inc(yt_done, 1)

                    for c in range(8):
                        rel_copy(g, 0, c)
                    rc_copy(g, 0, 0)
                    for i in range(NI):
                        for n in range(SLOTS):
                            if n < NH:
                                exp(g, i, n)
                            if n % 4 == 1 and n // 4 + 1 < QUADS:
                                rc_copy(g, i, n // 4 + 1)
                            if n % 4 == 3 and n >= 7 and (n - 7) // 4 < QUADS:
                                ct_copy(g, i, (n - 7) // 4)
                            if i + 1 < NI and n % 4 == 2 and n < NH:
                                rel_copy(g, i + 1, n // 4)
                            if i and n == 8:
                                yt_copy(g, i - 1)
                        if i + 1 < NI:
                            rc_copy(g, i + 1, 0)
                    yt_copy(g, NI - 1)

                @block.vector
                def _(dve):
                    def scores_min(g, i, n):
                        k = NH * i + n
                        wait(dve, qk_ready, k + 1)
                        start = 3e38
                        if i >= 2:
                            m = k - 2 * NH
                            nc.vector.tensor_reduce(fmin[:, i, n:n + 1], qk_ps[:, k % 2, 0:(i - 1) * P], AX.X,
                                                    ALU.min).then_inc(far_done, 1)
                            start = fmin[:, i, n:n + 1]
                        if n % 4 == 0:
                            wait(dve, near_done, k // 4 + 1)
                        if i >= 2:
                            wait(dve, far_done, m + 1)
                        lo = (i - 1) * P if i else 0
                        nb = near[:, k // 4 % 2, n % 4, 0:2, :] if i else near[:, k // 4 % 2, n % 4, 1:2, :]
                        s = qk_ps[:, k % 2, lo:(i + 1) * P]
                        nc.vector.tensor_tensor_reduce(out=s, in0=s, in1=nb.rearrange("p a b -> p (a b)"), scale=1.0,
                                                       scalar=start, op0=ALU.add, op1=ALU.min,
                                                       accum_out=nmin[:, i, n:n + 1]).then_inc(min_done, 1)

                    def pT_copy(g, i, n):
                        k = NH * (i - 1) + n
                        bank = bank_of["tp", i, n]
                        wait(dve, tp_ready, k + 1)
                        wait(dve, av_done, NH * i + n - 2)
                        nc.vector.tensor_copy(pT[:, k % 3, 0:(i + 1) * P], tp_ps[:, bank, 0:(i + 1) * P]).then_inc(pT_done, 1)

                    def rv_copy(g, i, half):
                        bank = bank_of["rv", i, half]
                        wait(dve, rv_ready, 2 * i + half + 1)
                        if half == 0:
                            wait(dve, rt_ready, i)
                        nc.vector.tensor_copy(rsb[:, 64 * half:64 * half + 64, :],
                                              g_ps[0:NH, bank, :].rearrange("p (t d) -> p t d", d=D)).then_inc(rsb_done, 1)

                    def normalise(g, i):
                        bank = bank_of["rt", i]
                        nc.vector.reciprocal(rden[:, :], den[:, i, :]).then_inc(y_chain, 1)
                        wait(dve, av_copied, i + 1)
                        wait(dve, rt_ready, i + 1)
                        nc.vector.tensor_tensor(ysum[:, :, :], av_sb[:, :].rearrange("p (n d) -> p n d", d=D),
                                                g_ps[:, bank, 0:NH * D].rearrange("p (d n) -> p n d", d=D),
                                                ALU.add).then_inc(y_chain, 1)
                        wait(dve, y_chain, 2 * i + 2)
                        wait(dve, yt_ready, i)
                        nc.vector.tensor_tensor(y[:, :, :], ysum[:, :, :],
                                                rden[:, :].unsqueeze(2).to_broadcast([P, NH, D]), ALU.mult).then_inc(y_done, 1)

                    def residual(g, i):
                        bank = bank_of["pj", i]
                        if i == 0:
                            wait(dve, xr_in, 16)
                        wait(dve, pj_ready, i + 1)
                        wait(dve, x1_out[i % 2], 16 * (i // 2))
                        nc.vector.tensor_tensor(x1[:, i % 2, :, :],
                                                g_ps[:, bank, 0:GB * C].rearrange("p (b c) -> p b c", b=GB),
                                                xr[:, :, :].rearrange("p (b i) c -> p b i c", b=GB)[:, :, i, :],
                                                ALU.add).then_inc(x1_done, 1)

                    for i in range(NI):
                        for n in range(SLOTS):
                            if n < NH:
                                scores_min(g, i, n)
                            if i and 0 <= n - 3 < NH:
                                pT_copy(g, i, n - 3)
                            if i and n == 4:
                                normalise(g, i - 1)
                            if i and n == 12:
                                residual(g, i - 1)
                        wait(dve, av_done, NH * (i + 1))
                        if i:
                            wait(dve, y_chain, 2 * i)
                        nc.vector.tensor_copy(av_sb[:, :], av_ps[:, 0:NH * D]).then_inc(av_copied, 1)
                        rv_copy(g, i, 0)
                        rv_copy(g, i, 1)
                    normalise(g, NI - 1)
                    residual(g, NI - 1)
            nc.all_engine_barrier(sems_to_clear=cleared)


def expert_part(nc, t, x1_dram, gate_w, gate_bias, w1, w3, w2, out):
    NM = NSH + E
    with ExitStack() as ctx:
        sb = lambda name, shape, dt: ctx.enter_context(nc.sbuf_tensor(name, shape, dt))
        sem = lambda name: ctx.enter_context(nc.semaphore(name))
        ps = lambda name, shape: ctx.enter_context(nc.psum_tensor(name, shape, F32))
        CT = CH // P
        NG = 4
        TURNS = 2
        CHUNKS = TILES // CT // TURNS
        LT = TILES // NG
        w1_sb = sb("w1_sb", [P, NM, P], F32)
        w3_sb = sb("w3_sb", [P, NM, P], F32)
        w2_sb = sb("w2_sb", [P, NM, P], F32)
        gw = sb("gw", [P, E], F32)
        gb = sb("gb", [P, E], F32)
        x1s = sb("x1s", [P, TILES, C], F32)
        xc = sb("xc2", [P, TILES, C], F32)
        sq = sb("sq2", [P, LT, C], F32)
        stat = sb("stat2", [P, 5, TILES], F32)
        rstd = sb("rstd2", [P, TILES], F32)
        xnT = sb("xnT2", [P, TILES * P], F32)
        order = sb("order", [P, E], F32)
        lg = sb("lg", [P, TILES, E], F32)
        score = sb("score", [P, TILES, E], F32)
        biased = sb("biased", [P, TILES, E], F32)
        pick = sb("pick", [P, 2, TILES, E], F32)
        tmp = sb("tmp", [P, TILES, E], F32)
        red = sb("red", [P, 8, TILES], F32)
        gates = sb("gates", [P, TILES, E], F32)
        gch = sb("gch", [P, 2, CT, E], F32)
        silu = sb("silu", [P, 2, CH], F32)
        hT = sb("hT", [P, 4, CH], F32)
        acc = sb("acc", [P, 2, CT, C], F32)
        h1_ps = ps("h1_ps", [P, 2, CH])
        h3_ps = ps("h3_ps", [P, 2, CH])
        y_ps = ps("y_ps", [P, 2, CH])
        xT_ps = ps("xT2_ps", [P, 512])
        lg_ps = ps("lg_ps", [P, 512])

        w_in = sem("w_in")
        x1_in = [sem(f"x1_in{n}") for n in range(NG)]
        chain = sem("chain2")
        xc_done = sem("xc2_done")
        sq_done = sem("sq2_done")
        sum_done = sem("sum2_done")
        var_done = sem("var2_done")
        sd_done = sem("sd2_done")
        xn_done = sem("xn2_done")
        xT_ready = sem("xT2_ready")
        xnT_done = sem("xnT2_done")
        lg_ready = sem("lg_ready")
        sh_done = sem("sh_done")
        ex_done = sem("ex_done")
        order_done = sem("order_done")
        gates_done = sem("gates_done")
        first = sem("first_of_loop")
        h1_ready = sem("h1_ready")
        h3_ready = sem("h3_ready")
        silu_done = sem("silu_done")
        hT_done = sem("hT_done")
        y_ready = sem("y_ready")
        acc_done = sem("acc_done")
        gch_done = sem("gch_done")
        out_done = [sem(f"out_done{n}") for n in range(2)]
        NU = E + 1
        AC = 1 + CT * E
        cleared = range(first.num, out_done[1].num + 1)

        def additions(k):
            return AC * (k // NU) + 1 + CT * (k % NU) if k >= 0 else 0

        x1_tiles = x1_dram.rearrange("b (i p) c -> p (b i) c", p=P)
        out_tiles = out.rearrange("b (i p) c -> p (b i) c", p=P)
        with nc.Block() as block:

            @block.sync
            def _(sp):
                for n in range(NG):
                    sp.dma_start(x1s[:, n * LT:(n + 1) * LT, :], x1_tiles[:, n * LT:(n + 1) * LT, :]).then_inc(x1_in[n], 16)
                for dst, src in ((gw[:, :], gate_w), (gb[:, :], gate_bias), (w1_sb[:, :, :], w1), (w3_sb[:, :, :], w3),
                                 (w2_sb[:, :, :], w2)):
                    sp.dma_start(dst, src).then_inc(w_in, 16)

            @block.gpsimd
            def _(pool):
                for e in range(E):
                    ins = nc.gpsimd.memset(order[:, e:e + 1], float(E - e))
                ins.then_inc(order_done, 1)

            @block.tensor
            def _(pe):
                for n in range(TILES // 4):
                    pe.wait_ge(xn_done, n // (LT // 4) + 1)
                    pe.wait_ge(xnT_done, n)
                    for q in range(4):
                        ins = nc.tensor.transpose(xT_ps[:, q * P:(q + 1) * P], xc[:, 4 * n + q, :], t["ident"][:, :])
                    ins.then_inc(xT_ready, 1)
                pe.wait_ge(w_in, 16 * 5)
                pe.wait_ge(xnT_done, TILES // 4)
                for n in range(TILES):
                    ins = nc.tensor.matmul(lg_ps[:, n * E:(n + 1) * E], xnT[:, n * P:(n + 1) * P], gw[:, :],
                                           start=True, stop=True)
                ins.then_inc(lg_ready, 1)

            @block.scalar
            def _(act):
                for n in range(NG):
                    act.wait_ge(xc_done, n + 1)
                    if n:
                        act.wait_ge(sum_done, n)
                    nc.scalar.activation(sq[:, :, :], xc[:, n * LT:(n + 1) * LT, :], ACT.Square).then_inc(sq_done, 1)
                act.wait_ge(var_done, 1)
                nc.scalar.activation(stat[:, 4, :], stat[:, 3, :], ACT.Sqrt).then_inc(sd_done, 1)
                for n in range(TILES // 4):
                    act.wait_ge(xT_ready, n + 1)
                    nc.scalar.activation(xnT[:, n * 512:(n + 1) * 512], xT_ps[:, :], ACT.Copy).then_inc(xnT_done, 1)
                act.wait_ge(sh_done, 1)
                nc.scalar.activation(score[:, :, :], lg[:, :, :], ACT.Exp).then_inc(ex_done, 1)

            @block.vector
            def _(dve):
                step = [0]

                def then(ins):
                    step[0] += 1
                    ins.then_inc(chain, 1)
                    dve.wait_ge(chain, step[0])

                for n in range(NG):
                    lot = slice(n * LT, (n + 1) * LT)
                    dve.wait_ge(x1_in[n], 16)
                    then(nc.vector.tensor_reduce(stat[:, 0, lot], x1s[:, lot, :], AX.X, ALU.add))
                    then(nc.vector.tensor_scalar(stat[:, 1, lot], stat[:, 0, lot], 1.0 / C, None, ALU.mult))
                    nc.vector.tensor_tensor(xc[:, lot, :], x1s[:, lot, :],
                                            stat[:, 1, lot].unsqueeze(2).to_broadcast([P, LT, C]),
                                            ALU.subtract).then_inc(xc_done, 1)
                    if n:
                        dve.wait_ge(sq_done, n)
                        nc.vector.tensor_reduce(stat[:, 2, (n - 1) * LT:n * LT], sq[:, :, :], AX.X,
                                                ALU.add).then_inc(sum_done, 1)
                dve.wait_ge(sq_done, NG)
                nc.vector.tensor_reduce(stat[:, 2, (NG - 1) * LT:NG * LT], sq[:, :, :], AX.X, ALU.add).then_inc(sum_done, 1)
                dve.wait_ge(sum_done, NG)
                nc.vector.tensor_scalar(stat[:, 3, :], stat[:, 2, :], 1.0 / C, EPS, ALU.mult, ALU.add).then_inc(var_done, 1)
                dve.wait_ge(sd_done, 1)
                then(nc.vector.reciprocal(rstd[:, :], stat[:, 4, :]))
                dve.wait_ge(xc_done, NG)
                for n in range(NG):
                    lot = slice(n * LT, (n + 1) * LT)
                    nc.vector.tensor_tensor(xc[:, lot, :], xc[:, lot, :],
                                            rstd[:, lot].unsqueeze(2).to_broadcast([P, LT, C]),
                                            ALU.mult).then_inc(xn_done, 1)

                wide = lambda r: red[:, r, :].unsqueeze(2).to_broadcast([P, TILES, E])
                rows = lambda v: v[:, :].unsqueeze(1).to_broadcast([P, TILES, E])
                lgp = lg_ps[:, 0:TILES * E].rearrange("p (n e) -> p n e", e=E)
                dve.wait_ge(lg_ready, 1)
                then(nc.vector.tensor_reduce(red[:, 0, :], lgp, AX.X, ALU.max))
                nc.vector.tensor_tensor(lg[:, :, :], lgp, wide(0), ALU.subtract).then_inc(sh_done, 1)
                dve.wait_ge(ex_done, 1)
                then(nc.vector.tensor_reduce(red[:, 1, :], score[:, :, :], AX.X, ALU.add))
                then(nc.vector.reciprocal(red[:, 2, :], red[:, 1, :]))
                then(nc.vector.tensor_tensor(score[:, :, :], score[:, :, :], wide(2), ALU.mult))
                dve.wait_ge(w_in, 16 * 5)
                then(nc.vector.tensor_tensor(biased[:, :, :], score[:, :, :], rows(gb), ALU.add))
                dve.wait_ge(order_done, 1)
                for r in range(TOPK):
                    then(nc.vector.tensor_reduce(red[:, 3 + 2 * r, :], biased[:, :, :], AX.X, ALU.max))
                    then(nc.vector.tensor_tensor(tmp[:, :, :], biased[:, :, :], wide(3 + 2 * r), ALU.is_equal))
                    then(nc.vector.tensor_tensor(tmp[:, :, :], tmp[:, :, :], rows(order), ALU.mult))
                    then(nc.vector.tensor_reduce(red[:, 4 + 2 * r, :], tmp[:, :, :], AX.X, ALU.max))
                    then(nc.vector.tensor_tensor(pick[:, r, :, :], tmp[:, :, :], wide(4 + 2 * r), ALU.is_equal))
                    if r + 1 < TOPK:
                        then(nc.vector.scalar_tensor_tensor(out=biased[:, :, :], in0=pick[:, r, :, :], scalar=-BIG,
                                                            in1=biased[:, :, :], op0=ALU.mult, op1=ALU.add))
                then(nc.vector.tensor_tensor(tmp[:, :, :], pick[:, 0, :, :], pick[:, 1, :, :], ALU.add))
                then(nc.vector.tensor_tensor(gates[:, :, :], score[:, :, :], tmp[:, :, :], ALU.mult))

        with nc.Fori(0, TURNS) as g:
            with nc.Block() as block:

                @block.sync
                def _(sp):
                    for c in range(CHUNKS):
                        sp.wait_ge(acc_done, (c + 1) * AC)
                        sp.dma_start(out_tiles[:, bass.ds((g * CHUNKS + c) * CT, CT), :],
                                     acc[:, c % 2, :, :]).then_inc(out_done[c % 2], 16)
                    for c in range(2):
                        sp.wait_ge(out_done[c], 16 * CHUNKS // 2)

                @block.tensor
                def _(pe):
                    def hidden(c, m):
                        k = NM * c + m
                        rhs = xnT[:, bass.ds((g * CHUNKS + c) * CH, CH)]
                        wait(pe, silu_done, k - 1)
                        wait(pe, hT_done, k - 1)
                        nc.tensor.matmul(h1_ps[:, k % 2, :], w1_sb[:, m, :], rhs, start=True,
                                         stop=True).then_inc(h1_ready, 1)
                        nc.tensor.matmul(h3_ps[:, k % 2, :], w3_sb[:, m, :], rhs, start=True,
                                         stop=True).then_inc(h3_ready, 1)

                    def product(c, u):
                        k = NU * c + u
                        ms = (0, 1) if u == 0 else (u + 1,)
                        pe.wait_ge(hT_done, NM * c + ms[-1] + 1)
                        wait(pe, acc_done, additions(k - 2))
                        for n in range(CT):
                            for m in ms:
                                ins = nc.tensor.matmul(y_ps[:, k % 2, n * P:(n + 1) * P],
                                                       hT[:, (NM * c + m) % 4, n * P:(n + 1) * P], w2_sb[:, m, :],
                                                       start=(m == ms[0]), stop=(m == ms[-1]))
                        ins.then_inc(y_ready, 1)

                    for c in range(CHUNKS):
                        for m in range(NM):
                            hidden(c, m)
                            if m >= 2:
                                product(c, m - 2)
                        product(c, NU - 1)

                @block.scalar
                def _(act):
                    for k in range(CHUNKS * NM):
                        act.wait_ge(h1_ready, k + 1)
                        wait(act, hT_done, k - 1)
                        nc.scalar.activation(silu[:, k % 2, :], h1_ps[:, k % 2, :], ACT.Silu).then_inc(silu_done, 1)

                @block.vector
                def _(dve):
                    def hidden(c, m):
                        k = NM * c + m
                        dve.wait_ge(silu_done, k + 1)
                        dve.wait_ge(h3_ready, k + 1)
                        if k >= 4:
                            cb, mb = divmod(k - 4, NM)
                            dve.wait_ge(y_ready, NU * cb + max(mb - 1, 0) + 1)
                        nc.vector.tensor_tensor(hT[:, k % 4, :], silu[:, k % 2, :], h3_ps[:, k % 2, :],
                                                ALU.mult).then_inc(hT_done, 1)

                    def add(c, u):
                        k = NU * c + u
                        dve.wait_ge(y_ready, k + 1)
                        if u == 0:
                            wait(dve, out_done[c % 2], 16 * (c // 2))
                            ys = y_ps[:, k % 2, :].rearrange("p (n c) -> p n c", c=C)
                            nc.vector.tensor_tensor(acc[:, c % 2, :, :], ys,
                                                    x1s[:, bass.ds((g * CHUNKS + c) * CT, CT), :],
                                                    ALU.add).then_inc(acc_done, 1)
                            return
                        for n in range(CT):
                            dve.wait_ge(acc_done, AC * c + 1 + (CT * (u - 2) + n + 1 if u > 1 else 0))
                            nc.vector.scalar_tensor_tensor(out=acc[:, c % 2, n, :],
                                                           in0=y_ps[:, k % 2, n * P:(n + 1) * P],
                                                           scalar=gch[:, c % 2, n, u - 1:u], in1=acc[:, c % 2, n, :],
                                                           op0=ALU.mult, op1=ALU.add).then_inc(acc_done, 1)

                    for c in range(CHUNKS):
                        wait(dve, acc_done, AC * (c - 1))
                        nc.vector.tensor_copy(gch[:, c % 2, :, :],
                                              gates[:, bass.ds((g * CHUNKS + c) * CT, CT), :]).then_inc(gch_done, 1)
                        dve.wait_ge(gch_done, c + 1)
                        for m in range(NM):
                            hidden(c, m)
                            if m >= 2:
                                add(c, m - 2)
                        add(c, NU - 1)

            nc.all_engine_barrier(sems_to_clear=cleared)


def block_kernel(nc, x, w_attn, w_proj, e_k, e_k127, e_k127h, e_v, e_v127, part_of_row, gate_w, gate_bias, w1, w3, w2,
                 out):
    q_parts = nc.dram_tensor("q_parts", [3, D, B, H, T], BF16, kind="Internal").ap()
    k_parts = nc.dram_tensor("k_parts", [3, D, B, H, T], BF16, kind="Internal").ap()
    v_dram = nc.dram_tensor("v_dram", [P, TILES, C], F32, kind="Internal").ap()
    x1_dram = nc.dram_tensor("x1_dram", [B, T, C], F32, kind="Internal").ap()
    with ExitStack() as ctx:
        sb = lambda name, shape, dt: ctx.enter_context(nc.sbuf_tensor(name, shape, dt))
        t = {"ident": sb("ident", [P, P], F32),
             "te": sb("te", [KR, 2 * NREL], BF16),
             "wp": sb("wp", [P, C], F32),
             "mask_far": sb("mask_far", [P, P], F32),
             "mask_big": sb("mask_big", [P, P], F32),
             "tv": sb("tv", [P, NREL, D], F32)}
        qkv_part(nc, t, x, w_attn, w_proj, e_k, e_k127, e_k127h, e_v, e_v127, part_of_row, q_parts, k_parts, v_dram)
        attention_part(nc, t, x, q_parts, k_parts, v_dram, x1_dram)
        expert_part(nc, t, x1_dram, gate_w, gate_bias, w1, w3, w2, out)


def kernel(**inputs):
    import concourse.bacc as bacc
    from concourse.bass_utils import run_bass_kernel_spmd

    a = {k[3:]: np.asarray(v) for k, v in inputs.items()}
    x, ek, ev = a["attn_x"], a["attn_embk"], a["attn_embv"]
    around = (-np.arange(2 * NREL)) % NREL
    turn = (np.arange(NREL)[None, :] - np.arange(P)[:, None]) % NREL
    hidden = lambda shared, experts: np.concatenate([shared.reshape(NSH, P, C), experts]).transpose(2, 0, 1)
    arrays = {
        "x": x,
        "w_attn": a["attn_w_attn"],
        "w_proj": a["attn_w_proj"],
        "e_k": np.tile(ek[around].T, (len(K_PART), 1)),
        "e_k127": np.tile(ek[-1], len(K_PART))[:, None],
        "e_k127h": np.tile(ek[-1], H)[:, None],
        "e_v": ev[turn],
        "e_v127": np.broadcast_to(np.tile(ev[-1], H), (P, C)),
        "part_of_row": np.repeat(np.eye(3, dtype=np.float32)[K_PART], D, axis=0),
        "gate_w": a["ffn_gate_w"].T,
        "gate_bias": np.broadcast_to(a["ffn_gate_bias"], (P, E)),
        "w1": hidden(a["ffn_sw1"], a["ffn_w1"]),
        "w3": hidden(a["ffn_sw3"], a["ffn_w3"]),
        "w2": np.concatenate([a["ffn_sw2"].T.reshape(NSH, P, C), a["ffn_w2"].transpose(0, 2, 1)]).transpose(1, 0, 2),
    }
    nc = bacc.Bacc("TRN2", target_bir_lowering=False, num_devices=1)
    feed, args = {}, []
    for name, v in arrays.items():
        v = np.ascontiguousarray(v)
        feed[f"in_{name}"] = v
        args.append(nc.dram_tensor(f"in_{name}", v.shape, mybir.dt.from_np(v.dtype), kind="ExternalInput").ap())
    args.append(nc.dram_tensor("out_0", x.shape, F32, kind="ExternalOutput").ap())
    block_kernel(nc, *args)
    r = run_bass_kernel_spmd(nc, [feed], core_ids=[0])
    return r.results[0]["out_0"]
```

```python
from contextlib import ExitStack

import numpy as np

import concourse.bass as bass
from concourse import mybir

F32 = mybir.dt.float32
BF16 = mybir.dt.bfloat16
ALU = mybir.AluOpType
ACT = mybir.ActivationFunctionType
AX = mybir.AxisListType

P = 128
B, T, C = 8, 512, 128
H, D = 16, 8
NI = T // P
NREL = 128
TILES = B * NI
SCALE = 1.0 / np.sqrt(np.float32(D))
EPS = 1e-5
BIG = 1e30

GB = 2
G = B // GB
NH = GB * H
QUADS = NH // 4
Q_PART = [0, 0, 1, 1, 2, 0]
K_PART = [0, 1, 0, 1, 0, 2]
KR = 8 * len(Q_PART)

E = 8
TOPK = 2
NSH = 2
CH = 512


SLOTS = NH + 7


def pe_slot(i, n):
    ops = []
    if n < NH:
        ops.append(("qk", i, n))
    if 0 <= n - 4 < NH:
        ops.append(("tp", i, n - 4))
    if n % 4 == 0 and n // 4 + 1 < QUADS:
        ops.append(("tr", i, n // 4 + 1))
    if i + 1 < NI and n % 4 == 2 and n < NH:
        ops.append(("rel", i + 1, n // 4))
    if n % 4 == 2 and n >= 10:
        ops.append(("av", i, (n - 10) // 4))
    if i and n == 1:
        ops.append(("rt", i - 1))
    if i and n == 5:
        ops.append(("dn", i - 1, 0))
    if i and n == 7:
        ops.append(("dn", i - 1, 1))
    if i and n == 11:
        ops.append(("pj", i - 1))
    return ops


ACT_COPIES = {0: (), 1: (), 2: (3, 7), 3: (2, 5, 7)}


def on_act(i, n):
    return n % 8 in ACT_COPIES[i]


def copies(engine_is_act, i, n):
    return sum(on_act(j, m) == engine_is_act for j in range(i + 1) for m in range(NH if j < i else n + 1))


def bank_plan():
    g_uses, t_uses = [], []
    for c in range(8):
        (t_uses if c % 2 else g_uses).append(("rel", 0, c))
    g_uses.append(("tr", 0, 0))
    for i in range(NI):
        for n in range(SLOTS):
            for op in pe_slot(i, n):
                if op[0] in ("rel", "tr", "dn", "pj"):
                    g_uses.append(op)
                if op[0] == "tp":
                    t_uses.append(op)
        if i + 1 < NI:
            g_uses.append(("tr", i + 1, 0))
        t_uses += [("rv", i, 0), ("rv", i, 1)]
    g_uses += [("dn", NI - 1, 0), ("dn", NI - 1, 1), ("pj", NI - 1)]
    bank, before = {}, {}
    for first, uses in ((0, g_uses), (2, t_uses)):
        bank |= {use: first + n % 2 for n, use in enumerate(uses)}
        before |= {use: uses[n - 2] for n, use in enumerate(uses) if n >= 2}
    return bank, before


def wait(engine, signal, n):
    if n > 0:
        engine.wait_ge(signal, n)


def qkv_part(nc, t, x, w_attn, w_proj, e_k, e_k127, e_k127h, e_v, e_v127, part_of_row, q_parts, k_parts, v_dram):
    with ExitStack() as ctx:
        sb = lambda name, shape, dt: ctx.enter_context(nc.sbuf_tensor(name, shape, dt))
        sem = lambda name: ctx.enter_context(nc.semaphore(name))
        ps = lambda name, shape: ctx.enter_context(nc.psum_tensor(name, shape, F32))
        GT = GB * NI
        w_sb = sb("w_attn_sb", [P, 3 * C], F32)
        xg = sb("xg", [P, GT, C], F32)
        xc = sb("xc", [P, GT, C], F32)
        sq = sb("sq", [P, GT, C], F32)
        xn = sb("xn", [P, GT, C], F32)
        stat = sb("stat", [P, 5, GT], F32)
        rstd = sb("rstd", [P, GT], F32)
        xnT = sb("xnT", [P, GT * P], F32)
        parts = sb("parts", [P, 2, 3, GT * P], BF16)
        k32 = sb("k32", [P, GT * P], F32)
        rest = sb("rest", [P, 2, GT * P], F32)
        vg = sb("vg", [P, GT, C], F32)
        ek = sb("ek", [KR, 2 * NREL], F32)
        ekr = sb("ekr", [KR, 2, 2 * NREL], F32)
        ekp = sb("ekp", [KR, 3, 2 * NREL], BF16)
        k127 = sb("k127", [KR, 1], F32)
        k127h = sb("k127h", [P, 1], F32)
        nk127h = sb("nk127h", [P, 1], F32)
        v127 = sb("v127", [P, C], F32)
        rowsel = sb("rowsel", [KR, 3], F32)
        xT_ps = ps("xT_ps", [P, 2, 512])
        q_ps = ps("q_ps", [P, 2, 512])
        k_ps = ps("k_ps", [P, 2, 512])
        v_ps = ps("v_ps", [P, 2, 512])

        const_in = sem("const_in")
        id_done = sem("id_done")
        x_in = sem("x_in")
        xc_done = sem("xc_done")
        sq_done = sem("sq_done")
        var_done = sem("var_done")
        sd_done = sem("sd_done")
        xn_done = sem("xn_done")
        xT_ready = sem("xT_ready")
        xnT_done = sem("xnT_done")
        q_ready = sem("q_ready")
        k_ready = sem("k_ready")
        v_ready = sem("v_ready")
        p1_done = sem("p1_done")
        k32_done = sem("k32_done")
        rest_done = sem("rest_done")
        p2_done = sem("p2_done")
        p3_done = sem("p3_done")
        vg_done = sem("vg_done")
        parts_out = sem("parts_out")
        chain = sem("chain")
        tab = sem("tab")

        x_tiles = x.rearrange("b (i p) c -> p (b i) c", p=P)
        v_tiles = v_dram
        NOUT = 2 * 3 * GB + 1
        NCHAIN = 4
        block = ctx.enter_context(nc.Block())

        @block.sync
        def _(sp):
            for dst, src in ((w_sb, w_attn), (ek, e_k), (k127, e_k127), (k127h, e_k127h), (v127, e_v127),
                             (rowsel, part_of_row)):
                sp.dma_start(dst[:, :], src).then_inc(const_in, 16)
            sp.dma_start(t["tv"][:, :, :], e_v).then_inc(const_in, 16)
            sp.dma_start(t["wp"][:, :, :], w_proj).then_inc(const_in, 16)
            for g in range(G):
                wait(sp, xc_done, g)
                sp.dma_start(xg[:, :, :], x_tiles[:, bass.ds(g * GT, GT), :]).then_inc(x_in, 16)
                for n, (dst, third) in enumerate(((q_parts, 0), (k_parts, 1))):
                    wait(sp, p3_done, 2 * g + 1 + n)
                    for m in range(3):
                        for b in range(GB):
                            src = parts[:, third, m, b * T:(b + 1) * T]
                            sp.dma_start(dst[m, :, bass.ds(g * GB + b, 1), :, :].rearrange("d a h t -> h d (a t)"),
                                         src).then_inc(parts_out, 16)
                wait(sp, vg_done, g + 1)
                sp.dma_start(v_tiles[:, bass.ds(g * GT, GT), :], vg[:, :, :]).then_inc(parts_out, 16)
            wait(sp, parts_out, 16 * NOUT * G)

        @block.gpsimd
        def _(pool):
            nc.gpsimd.memset(t["ident"][:, :], 0.0).then_inc(id_done, 1)
            wait(pool, id_done, 1)
            nc.gpsimd.affine_select(out=t["ident"][:, :], in_=t["ident"][:, :], compare_op=ALU.not_equal, fill=1.0,
                                    base=0, pattern=[[-1, P]], channel_multiplier=1).then_inc(id_done, 1)
            nc.gpsimd.memset(t["kb"][:, :, :], 0.0)
            nc.gpsimd.memset(t["qb"][:, :, :, :], 0.0)
            for g in range(G):
                for n in range(2):
                    wait(pool, p2_done, 2 * g + 1 + n)
                    nc.gpsimd.tensor_tensor(parts[:, n, 2, :], rest[:, n, :], parts[:, n, 1, :],
                                            ALU.subtract).then_inc(p3_done, 1)

        @block.tensor
        def _(pe):
            wait(pe, id_done, 2)
            wait(pe, const_in, 16 * 8)
            for g in range(G):
                wait(pe, xn_done, g + 1)
                wait(pe, xnT_done, 2 * g)
                for n in range(GT):
                    ins = nc.tensor.transpose(xT_ps[:, n // 4, (n % 4) * P:(n % 4 + 1) * P], xn[:, n, :],
                                              t["ident"][:, :])
                    if n % 4 == 3:
                        ins.then_inc(xT_ready, 1)
                wait(pe, xnT_done, 2 * g + 2)
                wait(pe, rest_done, 2 * g)
                for n in range(2):
                    nc.tensor.matmul(q_ps[:, n, :], w_sb[:, 0:C], xnT[:, n * 512:(n + 1) * 512],
                                     start=True, stop=True).then_inc(q_ready, 1)
                for n in range(2):
                    nc.tensor.matmul(k_ps[:, n, :], w_sb[:, C:2 * C], xnT[:, n * 512:(n + 1) * 512],
                                     start=True, stop=True).then_inc(k_ready, 1)
                wait(pe, vg_done, g)
                for n in range(GT):
                    ins = nc.tensor.matmul(v_ps[:, n // 4, (n % 4) * P:(n % 4 + 1) * P], xnT[:, n * P:(n + 1) * P],
                                           w_sb[:, 2 * C:3 * C], start=True, stop=True)
                ins.then_inc(v_ready, 1)

        @block.scalar
        def _(act):
            wait(act, tab, 2)
            for g in range(G):
                wait(act, xc_done, g + 1)
                nc.scalar.activation(sq[:, :, :], xc[:, :, :], ACT.Square).then_inc(sq_done, 1)
                wait(act, var_done, g + 1)
                nc.scalar.activation(stat[:, 4, :], stat[:, 3, :], ACT.Sqrt).then_inc(sd_done, 1)
                wait(act, v_ready, g)
                for n in range(2):
                    wait(act, xT_ready, 2 * g + 1 + n)
                    nc.scalar.activation(xnT[:, n * 512:(n + 1) * 512], xT_ps[:, n, :], ACT.Copy).then_inc(xnT_done, 1)
                wait(act, parts_out, g * 16 * NOUT)
                wait(act, q_ready, 2 * g + 2)
                nc.scalar.activation(parts[:, 0, 0, :], q_ps[:, :, :], ACT.Copy).then_inc(p1_done, 1)
                wait(act, k_ready, 2 * g + 2)
                nc.scalar.activation(k32[:, :], k_ps[:, :, :], ACT.Identity, bias=nk127h[:, 0:1],
                                     scale=-float(SCALE)).then_inc(k32_done, 1)
                wait(act, k32_done, g + 1)
                nc.scalar.activation(parts[:, 1, 0, :], k32[:, :], ACT.Copy).then_inc(p1_done, 1)
                for n in range(2):
                    wait(act, rest_done, 2 * g + 1 + n)
                    nc.scalar.activation(parts[:, n, 1, :], rest[:, n, :], ACT.Copy).then_inc(p2_done, 1)

        @block.vector
        def _(dve):
            wait(dve, const_in, 16 * 8)
            nc.vector.memset(t["te"][:, :], 0.0).then_inc(tab, 1)
            nc.vector.tensor_scalar(nk127h[:, :], k127h[:, :], -1.0, None, ALU.mult).then_inc(tab, 1)
            nc.vector.tensor_scalar(ekr[:, 0, :], ek[:, :], -1.0, k127[:, 0:1], ALU.mult, ALU.add).then_inc(tab, 1)
            wait(dve, tab, 3)
            nc.vector.tensor_tensor(t["tv"][:, :, :], t["tv"][:, :, :],
                                    v127[:, 0:D].unsqueeze(1).to_broadcast([P, NREL, D]), ALU.subtract).then_inc(tab, 1)
            nc.vector.tensor_copy(ekp[:, 0, :], ekr[:, 0, :]).then_inc(tab, 1)
            wait(dve, tab, 5)
            nc.vector.tensor_tensor(ekr[:, 1, :], ekr[:, 0, :], ekp[:, 0, :], ALU.subtract).then_inc(tab, 1)
            wait(dve, tab, 6)
            nc.vector.tensor_copy(ekp[:, 1, :], ekr[:, 1, :]).then_inc(tab, 1)
            wait(dve, tab, 7)
            nc.vector.tensor_tensor(ekp[:, 2, :], ekr[:, 1, :], ekp[:, 1, :], ALU.subtract).then_inc(tab, 1)
            wait(dve, tab, 8)
            nc.vector.tensor_scalar(ekr[:, 0, :], ekp[:, 0, :], rowsel[:, 0:1], None, ALU.mult).then_inc(tab, 1)
            wait(dve, tab, 9)
            nc.vector.scalar_tensor_tensor(out=ekr[:, 1, :], in0=ekp[:, 1, :], scalar=rowsel[:, 1:2],
                                           in1=ekr[:, 0, :], op0=ALU.mult, op1=ALU.add).then_inc(tab, 1)
            wait(dve, tab, 10)
            nc.vector.scalar_tensor_tensor(out=t["te"][0:KR, :], in0=ekp[:, 2, :], scalar=rowsel[:, 2:3],
                                           in1=ekr[:, 1, :], op0=ALU.mult, op1=ALU.add).then_inc(tab, 1)
            for g in range(G):
                wait(dve, x_in, 16 * (g + 1))
                nc.vector.tensor_reduce(stat[:, 0, :], xg[:, :, :], AX.X, ALU.add).then_inc(chain, 1)
                wait(dve, chain, NCHAIN * g + 1)
                nc.vector.tensor_scalar(stat[:, 1, :], stat[:, 0, :], 1.0 / C, None, ALU.mult).then_inc(chain, 1)
                wait(dve, chain, NCHAIN * g + 2)
                nc.vector.tensor_tensor(xc[:, :, :], xg[:, :, :],
                                        stat[:, 1, :].unsqueeze(2).to_broadcast([P, GT, C]),
                                        ALU.subtract).then_inc(xc_done, 1)
                wait(dve, sq_done, g + 1)
                nc.vector.tensor_reduce(stat[:, 2, :], sq[:, :, :], AX.X, ALU.add).then_inc(chain, 1)
                wait(dve, chain, NCHAIN * g + 3)
                nc.vector.tensor_scalar(stat[:, 3, :], stat[:, 2, :], 1.0 / C, EPS, ALU.mult,
                                        ALU.add).then_inc(var_done, 1)
                wait(dve, sd_done, g + 1)
                nc.vector.reciprocal(rstd[:, :], stat[:, 4, :]).then_inc(chain, 1)
                wait(dve, chain, NCHAIN * g + 4)
                wait(dve, xT_ready, 2 * g)
                wait(dve, xc_done, g + 1)
                nc.vector.tensor_tensor(xn[:, :, :], xc[:, :, :],
                                        rstd[:, :].unsqueeze(2).to_broadcast([P, GT, C]),
                                        ALU.mult).then_inc(xn_done, 1)
                wait(dve, p1_done, 2 * g + 1)
                nc.vector.tensor_tensor(rest[:, 0, :], q_ps[:, :, :].rearrange("p a n -> p (a n)"), parts[:, 0, 0, :],
                                        ALU.subtract).then_inc(rest_done, 1)
                wait(dve, p1_done, 2 * g + 2)
                nc.vector.tensor_tensor(rest[:, 1, :], k32[:, :], parts[:, 1, 0, :],
                                        ALU.subtract).then_inc(rest_done, 1)
                wait(dve, v_ready, g + 1)
                wait(dve, parts_out, g * 16 * NOUT)
                nc.vector.tensor_tensor(vg[:, :, :], v_ps[:, :, :].rearrange("p a (n c) -> p (a n) c", c=C),
                                        v127[:, :].unsqueeze(1).to_broadcast([P, GT, C]), ALU.add).then_inc(vg_done, 1)


def attention_part(nc, t, x, q_parts, k_parts, v_dram, x1_dram):
    bank_of, use_before = bank_plan()
    with ExitStack() as ctx:
        sb = lambda name, shape, dt: ctx.enter_context(nc.sbuf_tensor(name, shape, dt))
        ps = lambda name, shape: ctx.enter_context(nc.psum_tensor(name, shape, F32))
        signals = []

        def sem(name):
            signals.append(ctx.enter_context(nc.semaphore(name)))
            return signals[-1]

        ident, te, tv, wp = t["ident"], t["te"], t["tv"], t["wp"]
        kb, qb, vb = t["kb"], t["qb"], t["vb"]
        xr = sb("xr", [P, GB * NI, C], F32)
        relS = sb("relS", [P, 2, P, NH], F32)
        rc = sb("rc", [P, 2, 4, P], F32)
        near = sb("near", [P, 2, 4, NI, P], F32)
        nmin = sb("nmin", [P, NI, NH], F32)
        prob = sb("prob", [P, 3, 4, T], F32)
        pT = sb("pT", [P, 2, 4, T], F32)
        ptmp = sb("ptmp", [P, 4, P], F32)
        pcT = sb("pcT", [P, NH, P], F32)
        rsb = sb("rsb", [P, 32, NH], F32)
        av_sb = sb("av_sb", [P, GB, T], F32)
        den = sb("den", [P, NI, NH], F32)
        rden = sb("rden", [P, NH], F32)
        rden32 = sb("rden32", [P, NH * 32], F32)
        y = sb("y", [P, GB, T], F32)
        x1 = sb("x1", [P, 2, GB, C], F32)

        qk_ps = ps("qk_ps", [P, 2, 512])
        ring_ps = ps("ring_ps", [P, 4, 512])
        av_ps = ps("av_ps", [P, GB, 512])

        k_in = [sem(f"k_in{b}") for b in range(GB)]
        q_in = [sem(f"q_in{n}") for n in range(2)]
        v_in = sem("v_in")
        xr_in = sem("xr_in")
        rel_ready = sem("rel_ready")
        rel_done = sem("rel_done")
        tr_ready = sem("tr_ready")
        rc_done = sem("rc_done")
        near_done = sem("near_done")
        qk_ready = sem("qk_ready")
        min_done = sem("min_done")
        exp_done = sem("exp_done")
        tp_ready = sem("tp_ready")
        pTa_done = sem("pTa_done")
        pTv_done = sem("pTv_done")
        ptmp_done = sem("ptmp_done")
        pc_done = sem("pc_done")
        av_done = sem("av_done")
        rv_ready = sem("rv_ready")
        rsb_done = sem("rsb_done")
        rt_ready = sem("rt_ready")
        av_copied = sem("av_copied")
        rden32_done = sem("rden32_done")
        dn_ready = sem("dn_ready")
        rden_done = sem("rden_done")
        y_done = sem("y_done")
        pj_ready = sem("pj_ready")
        x1_done = sem("x1_done")
        x1_out = [sem(f"x1_out{n}") for n in range(2)]
        clear_done = ctx.enter_context(nc.semaphore("clear_done"))

        def copied(i, n):
            return (pTa_done if on_act(i, n) else pTv_done, copies(on_act(i, n), i, n))

        def wait_copied(engine, i, n):
            wait(engine, pTa_done, copies(True, i, n))
            wait(engine, pTv_done, copies(False, i, n))

        READ = {
            "rel": lambda i, c: (rel_done, 8 * i + c + 1),
            "tr": lambda i, u: (rc_done, QUADS * i + u + 1),
            "dn": lambda i, b: (y_done, GB * i + b + 1),
            "pj": lambda i: (x1_done, i + 1),
            "tp": copied,
            "rv": lambda i, half: (rsb_done, 2 * i + half + 1),
        }

        x_tiles = x.rearrange("b (i p) c -> p (b i) c", p=P)
        x1_tiles = x1_dram.rearrange("b (i p) c -> p b i c", p=P)
        cleared = range(min(q.num for q in signals), max(q.num for q in signals) + 1)

        with nc.Block() as block:

            @block.vector
            def _(dve):
                nc.vector.memset(av_ps[:, :, :], 0.0)
                nc.vector.memset(near[:, :, :, 0:NI - 2, :], 0.0)
                nc.vector.memset(ring_ps[:, :, :], 0.0).then_inc(clear_done, 1)
                dve.wait_ge(clear_done, 1)

        with nc.Fori(0, G) as g:
            with nc.Block() as block:

                @block.sync
                def _(sp):
                    def load_q(i):
                        wait(sp, qk_ready, NH * (i - 1))
                        for s, m in enumerate(Q_PART):
                            src = q_parts[m, :, bass.ds(g * GB, GB), :, i * P:(i + 1) * P]
                            sp.dma_start(qb[8 * s:8 * s + 8, i % 2, :, :],
                                         src.rearrange("d b h t -> d (b h) t")).then_inc(q_in[i % 2], 16)

                    def store(i):
                        sp.wait_ge(x1_done, i + 1)
                        sp.dma_start(x1_tiles[:, bass.ds(g * GB, GB), i, :],
                                     x1[:, i % 2, :, :]).then_inc(x1_out[i % 2], 16)

                    load_q(0)
                    for b in range(GB):
                        for s, m in enumerate(K_PART):
                            src = k_parts[m, :, bass.ds(g * GB + b, 1), :, :].rearrange("d a h t -> d (a h) t")
                            sp.dma_start(kb[8 * s:8 * s + 8, b * H:(b + 1) * H, :], src).then_inc(k_in[b], 16)
                    sp.dma_start(vb[:, :, :], v_dram[:, bass.ds(g * GB * NI, GB * NI), :]).then_inc(v_in, 16)
                    load_q(1)
                    sp.dma_start(xr[:, :, :], x_tiles[:, bass.ds(g * GB * NI, GB * NI), :]).then_inc(xr_in, 16)
                    load_q(2)
                    store(0)
                    load_q(3)
                    for i in range(1, NI):
                        store(i)
                    for n in range(2):
                        sp.wait_ge(x1_out[n], 16 * NI // 2)

                @block.gpsimd
                def _(pool):
                    def masks(i, u):
                        k = QUADS * i + u
                        pool.wait_ge(rc_done, k + 1)
                        wait(pool, min_done, 4 * (k - 1))
                        if i:
                            nc.gpsimd.affine_select(out=near[:, k % 2, :, NI - 2, :], in_=rc[:, k % 2, :, :],
                                                    compare_op=ALU.is_gt, fill=0.0, base=0, pattern=[[0, 4], [1, P]],
                                                    channel_multiplier=-1)
                        nc.gpsimd.affine_select(out=near[:, k % 2, :, NI - 1, :], in_=rc[:, k % 2, :, :],
                                                compare_op=ALU.is_ge, fill=BIG, base=0, pattern=[[0, 4], [-1, P]],
                                                channel_multiplier=1).then_inc(near_done, 1)

                    def near_probs(i, u):
                        k = QUADS * (i - 1) + u
                        wait_copied(pool, i, 4 * u + 3)
                        wait(pool, pc_done, k)
                        nc.gpsimd.affine_select(out=ptmp[:, :, :], in_=pT[:, u % 2, :, (i - 1) * P:i * P],
                                                compare_op=ALU.is_gt, fill=0.0, base=0, pattern=[[0, 4], [-1, P]],
                                                channel_multiplier=1).then_inc(ptmp_done, 1)
                        pool.wait_ge(ptmp_done, k + 1)
                        if u == 0:
                            pool.wait_ge(rv_ready, 2 * i)
                        nc.gpsimd.tensor_tensor(pcT[:, 4 * u:4 * u + 4, :], ptmp[:, :, :],
                                                pT[:, u % 2, :, i * P:(i + 1) * P], ALU.add).then_inc(pc_done, 1)

                    masks(0, 0)
                    for i in range(NI):
                        for n in range(SLOTS + 1):
                            if n % 4 == 2 and (n + 2) // 4 < QUADS:
                                masks(i, (n + 2) // 4)
                            if i and n % 4 == 1 and n >= 9 and (n - 9) // 4 < QUADS:
                                near_probs(i, (n - 9) // 4)
                        if i + 1 < NI:
                            masks(i + 1, 0)

                @block.tensor
                def _(pe):
                    def take(*use):
                        if use in use_before:
                            kind, *what = use_before[use]
                            pe.wait_ge(*READ[kind](*what))
                        return ring_ps[:, bank_of[use], :]

                    def rel(i, c):
                        if c == 0:
                            pe.wait_ge(q_in[i % 2], 96 * (i // 2 + 1))
                        bank = take("rel", i, c)
                        for a in range(16):
                            tau = 16 * c + a
                            ins = nc.tensor.matmul(bank[:, a * NH:(a + 1) * NH], te[:, P - tau:2 * P - tau],
                                                   qb[:, i % 2, :, tau], start=True, stop=True)
                        ins.then_inc(rel_ready, 1)

                    def tr(i, u):
                        if u == 0:
                            pe.wait_ge(rel_done, 8 * (i + 1))
                        bank = take("tr", i, u)
                        for q in range(4):
                            ins = nc.tensor.transpose(bank[:, q * P:(q + 1) * P], relS[:, i % 2, :, 4 * u + q], ident[:, :])
                        ins.then_inc(tr_ready, 1)

                    def qk(i, n):
                        k = NH * i + n
                        if i == 0 and n % H == 0:
                            pe.wait_ge(k_in[n // H], 96)
                        wait(pe, exp_done, k - 1)
                        nc.tensor.matmul(qk_ps[:, k % 2, 0:(i + 1) * P], qb[:, i % 2, n, :], kb[:, n, 0:(i + 1) * P],
                                         start=True, stop=True).then_inc(qk_ready, 1)

                    def tp(i, n):
                        k = NH * i + n
                        bank = take("tp", i, n)
                        pe.wait_ge(exp_done, k + 1)
                        for j in range(i + 1):
                            ins = nc.tensor.transpose(bank[:, j * P:(j + 1) * P],
                                                      prob[:, k // 4 % 3, n % 4, j * P:(j + 1) * P], ident[:, :])
                        ins.then_inc(tp_ready, 1)

                    def av(i, u):
                        if u == 0:
                            wait(pe, av_copied, GB * i)
                            if i == 0:
                                pe.wait_ge(v_in, 16)
                        wait_copied(pe, i, 4 * u + 3)
                        b, hq = divmod(4 * u, H)
                        for j in range(i + 1):
                            for q in range(4):
                                rhs = pT[:, u % 2, q, j * P:(j + 1) * P] if i else pcT[:, 4 * u + q, :]
                                ins = nc.tensor.matmul(av_ps[32 * q:32 * q + D, b, hq // 4 * P:(hq // 4 + 1) * P],
                                                       vb[:, b * NI + j, (hq + q) * D:(hq + q + 1) * D], rhs,
                                                       start=(hq == 0 and j == 0), stop=False, skip_group_check=True)
                        ins.then_inc(av_done, 1)

                    def rv(i, half):
                        if half == 0 and i:
                            pe.wait_ge(pc_done, QUADS * i)
                        if i == 0:
                            wait_copied(pe, 0, NH - 1)
                        bank = take("rv", i, half)
                        for a in range(16):
                            for tq in range(4):
                                tau = 32 * tq + 16 * half + a
                                ins = nc.tensor.matmul(bank[32 * tq:32 * tq + D, a * NH:(a + 1) * NH], tv[:, tau, :],
                                                       pcT[:, :, tau], start=True, stop=True)
                        ins.then_inc(rv_ready, 1)

                    def rt(i):
                        pe.wait_ge(rsb_done, 2 * (i + 1))
                        for b in range(GB):
                            for tq in range(4):
                                for q in range(4):
                                    dst = av_ps[32 * q:32 * q + D, b, :].rearrange("d (u t) -> d u t", t=P)
                                    ins = nc.tensor.matmul(
                                        dst[:, :, 32 * tq:32 * tq + 32], ident[:, 32 * tq:32 * tq + D],
                                        rsb[:, :, H * b + q:H * (b + 1):4].rearrange("p t u -> p u t"),
                                        start=False, stop=(tq == 3), skip_group_check=True)
                        ins.then_inc(rt_ready, 1)

                    def dn(i, b):
                        pe.wait_ge(rden32_done, i + 1)
                        bank = take("dn", i, b)
                        for u in range(4):
                            h = b * H + 4 * u
                            ins = nc.tensor.matmul(bank[:, u * P:(u + 1) * P], rden32[:, 32 * h:32 * (h + 4)],
                                                   ident[:, :], start=True, stop=True)
                        ins.then_inc(dn_ready, 1)

                    def pj(i):
                        pe.wait_ge(y_done, GB * (i + 1))
                        bank = take("pj", i)
                        for b in range(GB):
                            for u in range(4):
                                ins = nc.tensor.matmul(bank[:, b * C:(b + 1) * C], y[:, b, u * P:(u + 1) * P],
                                                       wp[:, u, :], start=(u == 0), stop=(u == 3))
                        ins.then_inc(pj_ready, 1)

                    do = {"rel": rel, "tr": tr, "qk": qk, "tp": tp, "av": av, "rt": rt, "dn": dn, "pj": pj}
                    for c in range(8):
                        rel(0, c)
                    tr(0, 0)
                    for i in range(NI):
                        for n in range(SLOTS):
                            for kind, *what in pe_slot(i, n):
                                do[kind](*what)
                        if i + 1 < NI:
                            tr(i + 1, 0)
                        rv(i, 0)
                        rv(i, 1)
                    rt(NI - 1)
                    dn(NI - 1, 0)
                    dn(NI - 1, 1)
                    pj(NI - 1)

                @block.scalar
                def _(act):
                    def rel_copy(i, c):
                        act.wait_ge(rel_ready, 8 * i + c + 1)
                        if c == 0:
                            wait(act, tr_ready, QUADS * (i - 1))
                        bank = ring_ps[:, bank_of["rel", i, c], :]
                        nc.scalar.activation(relS[:, i % 2, 16 * c:16 * (c + 1), :],
                                             bank.rearrange("p (t n) -> p t n", n=NH),
                                             ACT.Copy).then_inc(rel_done, 1)

                    def rc_copy(i, u):
                        k = QUADS * i + u
                        act.wait_ge(tr_ready, k + 1)
                        wait(act, near_done, k - 1)
                        nc.scalar.activation(rc[:, k % 2, :, :],
                                             ring_ps[:, bank_of["tr", i, u], :].rearrange("p (q t) -> p q t", t=P), ACT.Copy).then_inc(rc_done, 1)

                    def exp(i, n):
                        k = NH * i + n
                        if n % 4 == 0:
                            wait(act, tp_ready, k - 8)
                        act.wait_ge(min_done, k + 1)
                        nc.scalar.activation(prob[:, k // 4 % 3, n % 4, 0:(i + 1) * P], qk_ps[:, k % 2, 0:(i + 1) * P],
                                             ACT.Exp, bias=nmin[:, i, n:n + 1], scale=-1.0,
                                             accum_out=den[:, i, n:n + 1]).then_inc(exp_done, 1)

                    def pT_copy(i, n):
                        act.wait_ge(tp_ready, NH * i + n + 1)
                        if i:
                            wait(act, av_done, QUADS * i + n // 4 - 1)
                            wait(act, pc_done, QUADS * (i - 1) + n // 4 - 1)
                        dst = pT[:, n // 4 % 2, n % 4, 0:(i + 1) * P] if i else pcT[:, n, :]
                        nc.scalar.activation(dst, ring_ps[:, bank_of["tp", i, n], 0:(i + 1) * P],
                                             ACT.Copy).then_inc(pTa_done, 1)

                    def rsb_copy(i, half):
                        act.wait_ge(rv_ready, 2 * i + half + 1)
                        if half == 0:
                            wait(act, rt_ready, i)
                        nc.scalar.activation(rsb[:, 16 * half:16 * half + 16, :],
                                             ring_ps[:, bank_of["rv", i, half], :].rearrange("p (t n) -> p t n", n=NH),
                                             ACT.Copy).then_inc(rsb_done, 1)

                    def av_copy(i, b):
                        act.wait_ge(rt_ready, i + 1)
                        wait(act, y_done, GB * (i - 1) + b + 1)
                        nc.scalar.activation(av_sb[:, b, :], av_ps[:, b, :], ACT.Copy).then_inc(av_copied, 1)

                    for c in range(8):
                        rel_copy(0, c)
                    rc_copy(0, 0)
                    for i in range(NI):
                        for n in range(SLOTS):
                            if 0 <= n - 5 < NH and on_act(i, n - 5):
                                pT_copy(i, n - 5)
                            if n < NH:
                                exp(i, n)
                            if i and n in (2, 3):
                                av_copy(i - 1, n - 2)
                            if n % 4 == 1 and n // 4 + 1 < QUADS:
                                rc_copy(i, n // 4 + 1)
                            if i + 1 < NI and n % 4 == 3 and n < NH:
                                rel_copy(i + 1, n // 4)
                        if i + 1 < NI:
                            rc_copy(i + 1, 0)
                        rsb_copy(i, 0)
                        rsb_copy(i, 1)
                    av_copy(NI - 1, 0)
                    av_copy(NI - 1, 1)

                @block.vector
                def _(dve):
                    def scores_min(i, n):
                        k = NH * i + n
                        dve.wait_ge(qk_ready, k + 1)
                        if n % 4 == 0:
                            dve.wait_ge(near_done, k // 4 + 1)
                        nb = near[:, k // 4 % 2, n % 4, NI - 1 - i:NI, :]
                        nc.vector.tensor_tensor_reduce(out=qk_ps[:, k % 2, 0:(i + 1) * P],
                                                       in0=qk_ps[:, k % 2, 0:(i + 1) * P],
                                                       in1=nb.rearrange("p a b -> p (a b)"), scale=1.0, scalar=3e38,
                                                       op0=ALU.add, op1=ALU.min,
                                                       accum_out=nmin[:, i, n:n + 1]).then_inc(min_done, 1)

                    def pT_copy(i, n):
                        dve.wait_ge(tp_ready, NH * i + n + 1)
                        if i and n % 4 == 0:
                            wait(dve, av_done, QUADS * i + n // 4 - 1)
                            wait(dve, pc_done, QUADS * (i - 1) + n // 4 - 1)
                        nc.vector.tensor_copy(pT[:, n // 4 % 2, n % 4, 0:(i + 1) * P] if i else pcT[:, n, :],
                                              ring_ps[:, bank_of["tp", i, n], 0:(i + 1) * P]).then_inc(pTv_done, 1)

                    def invert(i):
                        dve.wait_ge(exp_done, NH * (i + 1))
                        nc.vector.reciprocal(rden[:, :], den[:, i, :]).then_inc(rden_done, 1)
                        wait(dve, dn_ready, GB * i)
                        dve.wait_ge(rden_done, i + 1)
                        nc.vector.tensor_copy(rden32[:, :].rearrange("p (h r) -> p h r", r=32),
                                              rden[:, :].unsqueeze(2).to_broadcast([P, NH, 32])).then_inc(rden32_done, 1)

                    def normalise(i, b):
                        dve.wait_ge(dn_ready, GB * i + b + 1)
                        dve.wait_ge(av_copied, GB * i + b + 1)
                        wait(dve, pj_ready, i)
                        nc.vector.tensor_tensor(y[:, b, :], av_sb[:, b, :], ring_ps[:, bank_of["dn", i, b], :],
                                                ALU.mult).then_inc(y_done, 1)

                    def residual(i):
                        if i == 0:
                            dve.wait_ge(xr_in, 16)
                        dve.wait_ge(pj_ready, i + 1)
                        wait(dve, x1_out[i % 2], 16 * (i // 2))
                        nc.vector.tensor_tensor(x1[:, i % 2, :, :],
                                                ring_ps[:, bank_of["pj", i], 0:GB * C].rearrange("p (b c) -> p b c", b=GB),
                                                xr[:, :, :].rearrange("p (b i) c -> p b i c", b=GB)[:, :, i, :],
                                                ALU.add).then_inc(x1_done, 1)

                    for i in range(NI):
                        for n in range(SLOTS):
                            if n < NH:
                                scores_min(i, n)
                            if 0 <= n - 5 < NH and not on_act(i, n - 5):
                                pT_copy(i, n - 5)
                            if n == NH:
                                invert(i)
                            if i and n == 6:
                                normalise(i - 1, 0)
                            if i and n == 8:
                                normalise(i - 1, 1)
                            if i and n == 12:
                                residual(i - 1)
                    normalise(NI - 1, 0)
                    normalise(NI - 1, 1)
                    residual(NI - 1)

            nc.all_engine_barrier(sems_to_clear=cleared)


def expert_part(nc, t, x1_dram, gate_w, gate_bias, w1, w3, w2, out):
    NM = NSH + E
    with ExitStack() as ctx:
        sb = lambda name, shape, dt: ctx.enter_context(nc.sbuf_tensor(name, shape, dt))
        sem = lambda name: ctx.enter_context(nc.semaphore(name))
        ps = lambda name, shape: ctx.enter_context(nc.psum_tensor(name, shape, F32))
        CT = CH // P
        NG = 4
        TURNS = 2
        CHUNKS = TILES // CT // TURNS
        LT = TILES // NG
        w1_sb = sb("w1_sb", [P, NM, P], F32)
        w3_sb = sb("w3_sb", [P, NM, P], F32)
        w2_sb = sb("w2_sb", [P, NM, P], F32)
        gw = sb("gw", [P, E], F32)
        gb = sb("gb", [P, E], F32)
        x1s = sb("x1s", [P, TILES, C], F32)
        xc = sb("xc2", [P, TILES, C], F32)
        sq = sb("sq2", [P, LT, C], F32)
        stat = sb("stat2", [P, 5, TILES], F32)
        rstd = sb("rstd2", [P, TILES], F32)
        xnT = sb("xnT2", [P, TILES * P], F32)
        order = sb("order", [P, E], F32)
        lg = sb("lg", [P, TILES, E], F32)
        score = sb("score", [P, TILES, E], F32)
        biased = sb("biased", [P, TILES, E], F32)
        pick = sb("pick", [P, 2, TILES, E], F32)
        tmp = sb("tmp", [P, TILES, E], F32)
        red = sb("red", [P, 8, TILES], F32)
        gates = sb("gates", [P, TILES, E], F32)
        gch = sb("gch", [P, 2, CT, E], F32)
        silu = sb("silu", [P, 2, CH], F32)
        hT = sb("hT", [P, 4, CH], F32)
        acc = sb("acc", [P, 2, CT, C], F32)
        h1_ps = ps("h1_ps", [P, 2, CH])
        h3_ps = ps("h3_ps", [P, 2, CH])
        y_ps = ps("y_ps", [P, 2, CH])
        xT_ps = ps("xT2_ps", [P, 512])
        lg_ps = ps("lg_ps", [P, 512])

        w_in = sem("w_in")
        x1_in = [sem(f"x1_in{n}") for n in range(NG)]
        chain = sem("chain2")
        xc_done = sem("xc2_done")
        sq_done = sem("sq2_done")
        sum_done = sem("sum2_done")
        var_done = sem("var2_done")
        sd_done = sem("sd2_done")
        xn_done = sem("xn2_done")
        xT_ready = sem("xT2_ready")
        xnT_done = sem("xnT2_done")
        lg_ready = sem("lg_ready")
        sh_done = sem("sh_done")
        ex_done = sem("ex_done")
        order_done = sem("order_done")
        gates_done = sem("gates_done")
        first = sem("first_of_loop")
        h1_ready = sem("h1_ready")
        h3_ready = sem("h3_ready")
        silu_done = sem("silu_done")
        hT_done = sem("hT_done")
        y_ready = sem("y_ready")
        acc_done = sem("acc_done")
        gch_done = sem("gch_done")
        out_done = [sem(f"out_done{n}") for n in range(2)]
        NU = E + 1
        AC = 1 + CT * E
        cleared = range(first.num, out_done[1].num + 1)

        def additions(k):
            return AC * (k // NU) + 1 + CT * (k % NU) if k >= 0 else 0

        x1_tiles = x1_dram.rearrange("b (i p) c -> p (b i) c", p=P)
        out_tiles = out.rearrange("b (i p) c -> p (b i) c", p=P)
        with nc.Block() as block:

            @block.sync
            def _(sp):
                for n in range(NG):
                    sp.dma_start(x1s[:, n * LT:(n + 1) * LT, :], x1_tiles[:, n * LT:(n + 1) * LT, :]).then_inc(x1_in[n], 16)
                for dst, src in ((gw[:, :], gate_w), (gb[:, :], gate_bias), (w1_sb[:, :, :], w1), (w3_sb[:, :, :], w3),
                                 (w2_sb[:, :, :], w2)):
                    sp.dma_start(dst, src).then_inc(w_in, 16)

            @block.gpsimd
            def _(pool):
                for e in range(E):
                    ins = nc.gpsimd.memset(order[:, e:e + 1], float(E - e))
                ins.then_inc(order_done, 1)

            @block.tensor
            def _(pe):
                for n in range(TILES // 4):
                    pe.wait_ge(xn_done, n // (LT // 4) + 1)
                    pe.wait_ge(xnT_done, n)
                    for q in range(4):
                        ins = nc.tensor.transpose(xT_ps[:, q * P:(q + 1) * P], xc[:, 4 * n + q, :], t["ident"][:, :])
                    ins.then_inc(xT_ready, 1)
                pe.wait_ge(w_in, 16 * 5)
                pe.wait_ge(xnT_done, TILES // 4)
                for n in range(TILES):
                    ins = nc.tensor.matmul(lg_ps[:, n * E:(n + 1) * E], xnT[:, n * P:(n + 1) * P], gw[:, :],
                                           start=True, stop=True)
                ins.then_inc(lg_ready, 1)

            @block.scalar
            def _(act):
                for n in range(NG):
                    act.wait_ge(xc_done, n + 1)
                    if n:
                        act.wait_ge(sum_done, n)
                    nc.scalar.activation(sq[:, :, :], xc[:, n * LT:(n + 1) * LT, :], ACT.Square).then_inc(sq_done, 1)
                act.wait_ge(var_done, 1)
                nc.scalar.activation(stat[:, 4, :], stat[:, 3, :], ACT.Sqrt).then_inc(sd_done, 1)
                for n in range(TILES // 4):
                    act.wait_ge(xT_ready, n + 1)
                    nc.scalar.activation(xnT[:, n * 512:(n + 1) * 512], xT_ps[:, :], ACT.Copy).then_inc(xnT_done, 1)
                act.wait_ge(sh_done, 1)
                nc.scalar.activation(score[:, :, :], lg[:, :, :], ACT.Exp).then_inc(ex_done, 1)

            @block.vector
            def _(dve):
                step = [0]

                def then(ins):
                    step[0] += 1
                    ins.then_inc(chain, 1)
                    dve.wait_ge(chain, step[0])

                for n in range(NG):
                    lot = slice(n * LT, (n + 1) * LT)
                    dve.wait_ge(x1_in[n], 16)
                    then(nc.vector.tensor_reduce(stat[:, 0, lot], x1s[:, lot, :], AX.X, ALU.add))
                    then(nc.vector.tensor_scalar(stat[:, 1, lot], stat[:, 0, lot], 1.0 / C, None, ALU.mult))
                    nc.vector.tensor_tensor(xc[:, lot, :], x1s[:, lot, :],
                                            stat[:, 1, lot].unsqueeze(2).to_broadcast([P, LT, C]),
                                            ALU.subtract).then_inc(xc_done, 1)
                    if n:
                        dve.wait_ge(sq_done, n)
                        nc.vector.tensor_reduce(stat[:, 2, (n - 1) * LT:n * LT], sq[:, :, :], AX.X,
                                                ALU.add).then_inc(sum_done, 1)
                dve.wait_ge(sq_done, NG)
                nc.vector.tensor_reduce(stat[:, 2, (NG - 1) * LT:NG * LT], sq[:, :, :], AX.X, ALU.add).then_inc(sum_done, 1)
                dve.wait_ge(sum_done, NG)
                nc.vector.tensor_scalar(stat[:, 3, :], stat[:, 2, :], 1.0 / C, EPS, ALU.mult, ALU.add).then_inc(var_done, 1)
                dve.wait_ge(sd_done, 1)
                then(nc.vector.reciprocal(rstd[:, :], stat[:, 4, :]))
                dve.wait_ge(xc_done, NG)
                for n in range(NG):
                    lot = slice(n * LT, (n + 1) * LT)
                    nc.vector.tensor_tensor(xc[:, lot, :], xc[:, lot, :],
                                            rstd[:, lot].unsqueeze(2).to_broadcast([P, LT, C]),
                                            ALU.mult).then_inc(xn_done, 1)

                wide = lambda r: red[:, r, :].unsqueeze(2).to_broadcast([P, TILES, E])
                rows = lambda v: v[:, :].unsqueeze(1).to_broadcast([P, TILES, E])
                lgp = lg_ps[:, 0:TILES * E].rearrange("p (n e) -> p n e", e=E)
                dve.wait_ge(lg_ready, 1)
                then(nc.vector.tensor_reduce(red[:, 0, :], lgp, AX.X, ALU.max))
                nc.vector.tensor_tensor(lg[:, :, :], lgp, wide(0), ALU.subtract).then_inc(sh_done, 1)
                dve.wait_ge(ex_done, 1)
                then(nc.vector.tensor_reduce(red[:, 1, :], score[:, :, :], AX.X, ALU.add))
                then(nc.vector.reciprocal(red[:, 2, :], red[:, 1, :]))
                then(nc.vector.tensor_tensor(score[:, :, :], score[:, :, :], wide(2), ALU.mult))
                dve.wait_ge(w_in, 16 * 5)
                then(nc.vector.tensor_tensor(biased[:, :, :], score[:, :, :], rows(gb), ALU.add))
                dve.wait_ge(order_done, 1)
                for r in range(TOPK):
                    then(nc.vector.tensor_reduce(red[:, 3 + 2 * r, :], biased[:, :, :], AX.X, ALU.max))
                    then(nc.vector.tensor_tensor(tmp[:, :, :], biased[:, :, :], wide(3 + 2 * r), ALU.is_equal))
                    then(nc.vector.tensor_tensor(tmp[:, :, :], tmp[:, :, :], rows(order), ALU.mult))
                    then(nc.vector.tensor_reduce(red[:, 4 + 2 * r, :], tmp[:, :, :], AX.X, ALU.max))
                    then(nc.vector.tensor_tensor(pick[:, r, :, :], tmp[:, :, :], wide(4 + 2 * r), ALU.is_equal))
                    if r + 1 < TOPK:
                        then(nc.vector.scalar_tensor_tensor(out=biased[:, :, :], in0=pick[:, r, :, :], scalar=-BIG,
                                                            in1=biased[:, :, :], op0=ALU.mult, op1=ALU.add))
                then(nc.vector.tensor_tensor(tmp[:, :, :], pick[:, 0, :, :], pick[:, 1, :, :], ALU.add))
                then(nc.vector.tensor_tensor(gates[:, :, :], score[:, :, :], tmp[:, :, :], ALU.mult))

        with nc.Fori(0, TURNS) as g:
            with nc.Block() as block:

                @block.sync
                def _(sp):
                    for c in range(CHUNKS):
                        sp.wait_ge(acc_done, (c + 1) * AC)
                        sp.dma_start(out_tiles[:, bass.ds((g * CHUNKS + c) * CT, CT), :],
                                     acc[:, c % 2, :, :]).then_inc(out_done[c % 2], 16)
                    for c in range(2):
                        sp.wait_ge(out_done[c], 16 * CHUNKS // 2)

                @block.tensor
                def _(pe):
                    def hidden(c, m):
                        k = NM * c + m
                        rhs = xnT[:, bass.ds((g * CHUNKS + c) * CH, CH)]
                        wait(pe, silu_done, k - 1)
                        wait(pe, hT_done, k - 1)
                        nc.tensor.matmul(h1_ps[:, k % 2, :], w1_sb[:, m, :], rhs, start=True,
                                         stop=True).then_inc(h1_ready, 1)
                        nc.tensor.matmul(h3_ps[:, k % 2, :], w3_sb[:, m, :], rhs, start=True,
                                         stop=True).then_inc(h3_ready, 1)

                    def product(c, u):
                        k = NU * c + u
                        ms = (0, 1) if u == 0 else (u + 1,)
                        pe.wait_ge(hT_done, NM * c + ms[-1] + 1)
                        wait(pe, acc_done, additions(k - 2))
                        for n in range(CT):
                            for m in ms:
                                ins = nc.tensor.matmul(y_ps[:, k % 2, n * P:(n + 1) * P],
                                                       hT[:, (NM * c + m) % 4, n * P:(n + 1) * P], w2_sb[:, m, :],
                                                       start=(m == ms[0]), stop=(m == ms[-1]))
                        ins.then_inc(y_ready, 1)

                    for c in range(CHUNKS):
                        for m in range(NM):
                            hidden(c, m)
                            if m >= 2:
                                product(c, m - 2)
                        product(c, NU - 1)

                @block.scalar
                def _(act):
                    for k in range(CHUNKS * NM):
                        act.wait_ge(h1_ready, k + 1)
                        wait(act, hT_done, k - 1)
                        nc.scalar.activation(silu[:, k % 2, :], h1_ps[:, k % 2, :], ACT.Silu).then_inc(silu_done, 1)

                @block.vector
                def _(dve):
                    def hidden(c, m):
                        k = NM * c + m
                        dve.wait_ge(silu_done, k + 1)
                        dve.wait_ge(h3_ready, k + 1)
                        if k >= 4:
                            cb, mb = divmod(k - 4, NM)
                            dve.wait_ge(y_ready, NU * cb + max(mb - 1, 0) + 1)
                        nc.vector.tensor_tensor(hT[:, k % 4, :], silu[:, k % 2, :], h3_ps[:, k % 2, :],
                                                ALU.mult).then_inc(hT_done, 1)

                    def add(c, u):
                        k = NU * c + u
                        dve.wait_ge(y_ready, k + 1)
                        if u == 0:
                            wait(dve, out_done[c % 2], 16 * (c // 2))
                            ys = y_ps[:, k % 2, :].rearrange("p (n c) -> p n c", c=C)
                            nc.vector.tensor_tensor(acc[:, c % 2, :, :], ys,
                                                    x1s[:, bass.ds((g * CHUNKS + c) * CT, CT), :],
                                                    ALU.add).then_inc(acc_done, 1)
                            return
                        for n in range(CT):
                            dve.wait_ge(acc_done, AC * c + 1 + (CT * (u - 2) + n + 1 if u > 1 else 0))
                            nc.vector.scalar_tensor_tensor(out=acc[:, c % 2, n, :],
                                                           in0=y_ps[:, k % 2, n * P:(n + 1) * P],
                                                           scalar=gch[:, c % 2, n, u - 1:u], in1=acc[:, c % 2, n, :],
                                                           op0=ALU.mult, op1=ALU.add).then_inc(acc_done, 1)

                    for c in range(CHUNKS):
                        wait(dve, acc_done, AC * (c - 1))
                        nc.vector.tensor_copy(gch[:, c % 2, :, :],
                                              gates[:, bass.ds((g * CHUNKS + c) * CT, CT), :]).then_inc(gch_done, 1)
                        dve.wait_ge(gch_done, c + 1)
                        for m in range(NM):
                            hidden(c, m)
                            if m >= 2:
                                add(c, m - 2)
                        add(c, NU - 1)

            nc.all_engine_barrier(sems_to_clear=cleared)


def block_kernel(nc, x, w_attn, w_proj, e_k, e_k127, e_k127h, e_v, e_v127, part_of_row, gate_w, gate_bias, w1, w3, w2,
                 out):
    q_parts = nc.dram_tensor("q_parts", [3, D, B, H, T], BF16, kind="Internal").ap()
    k_parts = nc.dram_tensor("k_parts", [3, D, B, H, T], BF16, kind="Internal").ap()
    v_dram = nc.dram_tensor("v_dram", [P, TILES, C], F32, kind="Internal").ap()
    x1_dram = nc.dram_tensor("x1_dram", [B, T, C], F32, kind="Internal").ap()
    with ExitStack() as ctx:
        sb = lambda name, shape, dt: ctx.enter_context(nc.sbuf_tensor(name, shape, dt))
        t = {"ident": sb("ident", [P, P], F32),
             "te": sb("te", [P, 2 * NREL], BF16),
             "tv": sb("tv", [P, NREL, D], F32),
             "wp": sb("wp", [P, 4, C], F32),
             "kb": sb("kb", [P, NH, T], BF16),
             "qb": sb("qb", [P, 2, NH, P], BF16),
             "vb": sb("vb", [P, GB * NI, C], F32)}
        qkv_part(nc, t, x, w_attn, w_proj, e_k, e_k127, e_k127h, e_v, e_v127, part_of_row, q_parts, k_parts, v_dram)
        attention_part(nc, t, x, q_parts, k_parts, v_dram, x1_dram)
        expert_part(nc, t, x1_dram, gate_w, gate_bias, w1, w3, w2, out)


def kernel(**inputs):
    import concourse.bacc as bacc
    from concourse.bass_utils import run_bass_kernel_spmd

    a = {k[3:]: np.asarray(v) for k, v in inputs.items()}
    x, ek, ev = a["attn_x"], a["attn_embk"], a["attn_embv"]
    around = (-np.arange(2 * NREL)) % NREL
    turn = (np.arange(NREL)[None, :] - np.arange(P)[:, None]) % NREL
    hidden = lambda shared, experts: np.concatenate([shared.reshape(NSH, P, C), experts]).transpose(2, 0, 1)
    w_proj = np.zeros((4, 32, 4, C), np.float32)
    w_proj[:, :D] = a["attn_w_proj"].reshape(4, 4, D, C).transpose(1, 2, 0, 3)
    arrays = {
        "x": x,
        "w_attn": a["attn_w_attn"],
        "w_proj": w_proj.reshape(P, 4, C),
        "e_k": np.tile(ek[around].T, (len(K_PART), 1)),
        "e_k127": np.tile(ek[-1], len(K_PART))[:, None],
        "e_k127h": np.tile(ek[-1], H)[:, None],
        "e_v": ev[turn],
        "e_v127": np.broadcast_to(np.tile(ev[-1], H), (P, C)),
        "part_of_row": np.repeat(np.eye(3, dtype=np.float32)[K_PART], D, axis=0),
        "gate_w": a["ffn_gate_w"].T,
        "gate_bias": np.broadcast_to(a["ffn_gate_bias"], (P, E)),
        "w1": hidden(a["ffn_sw1"], a["ffn_w1"]),
        "w3": hidden(a["ffn_sw3"], a["ffn_w3"]),
        "w2": np.concatenate([a["ffn_sw2"].T.reshape(NSH, P, C), a["ffn_w2"].transpose(0, 2, 1)]).transpose(1, 0, 2),
    }
    nc = bacc.Bacc("TRN2", target_bir_lowering=False, num_devices=1)
    feed, args = {}, []
    for name, v in arrays.items():
        v = np.ascontiguousarray(v)
        feed[f"in_{name}"] = v
        args.append(nc.dram_tensor(f"in_{name}", v.shape, mybir.dt.from_np(v.dtype), kind="ExternalInput").ap())
    args.append(nc.dram_tensor("out_0", x.shape, F32, kind="ExternalOutput").ap())
    block_kernel(nc, *args)
    r = run_bass_kernel_spmd(nc, [feed], core_ids=[0])
    return r.results[0]["out_0"]
```

```python
from contextlib import ExitStack

import numpy as np

import concourse.bass as bass
from concourse import mybir

F32 = mybir.dt.float32
BF16 = mybir.dt.bfloat16
ALU = mybir.AluOpType
ACT = mybir.ActivationFunctionType
AX = mybir.AxisListType

P = 128
B, T, C = 8, 512, 128
H, D = 16, 8
NI = T // P
NREL = 128
TILES = B * NI
SCALE = 1.0 / np.sqrt(np.float32(D))
EPS = 1e-5
BIG = 1e30

GB = 2
G = B // GB
NH = GB * H
QUADS = NH // 4
Q_PART = [0, 0, 1, 1, 2, 0]
K_PART = [0, 1, 0, 1, 0, 2]
KR = 8 * len(Q_PART)

E = 8
TOPK = 2
NSH = 2
CH = 512


HEADS = NI * NH
SLOTS = HEADS + 32
RVN = 4

REL_AT = (5, 6, 9, 10, 13, 14, 17, 18)
RV_AT = (11, 15, 19, 21)
RT_AT = (22, 23)
DN_AT = (25, 26)
PJ_AT = 29


def pe_slot(s):
    i, n = divmod(s, NH)
    ops = []
    if s < HEADS:
        ops.append(("qk", i, n))
    if 0 <= s - 4 < HEADS:
        ops.append(("tp", *divmod(s - 4, NH)))
    if s % 4 == 0 and s + 4 <= HEADS:
        ops.append(("tr", *divmod(s // 4 + 1, QUADS)))
    if s % 4 == 2 and 0 <= s - 10 < HEADS:
        ops.append(("av", *divmod((s - 10) // 4, QUADS)))
    if i < NI and n in REL_AT:
        ops.append(("rel", i + 1, REL_AT.index(n)))
    if i:
        for kind, at in (("rv", RV_AT), ("rt", RT_AT), ("dn", DN_AT)):
            if n in at:
                ops.append((kind, i - 1, at.index(n)))
        if n == PJ_AT:
            ops.append(("pj", i - 1))
    return ops


ACT_COPIES = {0: (), 1: (), 2: (3, 7), 3: (2, 5, 7)}


def on_act(i, n):
    return n % 8 in ACT_COPIES[i]


def copies(engine_is_act, i, n):
    return sum(on_act(j, m) == engine_is_act for j in range(i + 1) for m in range(NH if j < i else n + 1))


def bank_plan():
    g_uses, t_uses = [], []
    for s in range(SLOTS):
        for op in pe_slot(s):
            if op[0] in ("rel", "tr", "rv", "rt", "dn", "pj"):
                g_uses.append(op)
            if op[0] == "tp":
                t_uses.append(op)
    bank, before = {}, {}
    for first, uses in ((0, g_uses), (2, t_uses)):
        bank |= {use: first + n % 2 for n, use in enumerate(uses)}
        before |= {use: uses[n - 2] for n, use in enumerate(uses) if n >= 2}
    return bank, before


def wait(engine, signal, n):
    if n > 0:
        engine.wait_ge(signal, n)


def qkv_part(nc, t, x, w_attn, w_proj, e_k, e_k127, e_k127h, e_v, e_v127, part_of_row, q_parts, k_parts, v_dram):
    with ExitStack() as ctx:
        sb = lambda name, shape, dt: ctx.enter_context(nc.sbuf_tensor(name, shape, dt))
        sem = lambda name: ctx.enter_context(nc.semaphore(name))
        ps = lambda name, shape: ctx.enter_context(nc.psum_tensor(name, shape, F32))
        GT = GB * NI
        w_sb = sb("w_attn_sb", [P, 3 * C], F32)
        xs = sb("xs", [P, TILES, C], F32)
        sq = sb("sq", [P, GT, C], F32)
        stat = sb("stat", [P, 5, TILES], F32)
        rstd = sb("rstd", [P, TILES], F32)
        xnT = sb("xnT", [P, 2, GT * P], F32)
        parts = sb("parts", [P, 2, 2, 3, GT * P], BF16)
        k32 = sb("k32", [P, 2, GT * P], F32)
        rest = sb("rest", [P, 2, 2, GT * P], F32)
        vg = sb("vg", [P, 2, GT, C], F32)
        ek = sb("ek", [KR, 2 * NREL], F32)
        ekr = sb("ekr", [KR, 2, 2 * NREL], F32)
        ekp = sb("ekp", [KR, 3, 2 * NREL], BF16)
        k127 = sb("k127", [KR, 1], F32)
        k127h = sb("k127h", [P, 1], F32)
        nk127h = sb("nk127h", [P, 1], F32)
        v127 = sb("v127", [P, C], F32)
        rowsel = sb("rowsel", [KR, 3], F32)
        xT_ps = ps("xT_ps", [P, 2, 512])
        q_ps = ps("q_ps", [P, 2, 512])
        k_ps = ps("k_ps", [P, 2, 512])
        v_ps = ps("v_ps", [P, 2, 512])

        w_in = sem("w_in")
        vec_in = sem("vec_in")
        tab_in = sem("tab_in")
        wp_in = sem("wp_in")
        bias_done = sem("bias_done")
        id_done = sem("id_done")
        x_in = [sem(f"x_in{g}") for g in range(G)]
        sum_done = sem("sum_done")
        mean_done = sem("mean_done")
        xc_done = sem("xc_done")
        sq_done = sem("sq_done")
        ssq_done = sem("ssq_done")
        var_done = sem("var_done")
        sd_done = sem("sd_done")
        rstd_done = sem("rstd_done")
        xn_done = sem("xn_done")
        xT_ready = sem("xT_ready")
        xnT_done = sem("xnT_done")
        q_ready = sem("q_ready")
        k_ready = sem("k_ready")
        v_ready = sem("v_ready")
        p1_done = sem("p1_done")
        k32_done = sem("k32_done")
        rest_done = sem("rest_done")
        p2_done = sem("p2_done")
        p3_done = sem("p3_done")
        vg_done = sem("vg_done")
        out_done = [sem(f"out_done{n}") for n in range(2)]
        tab = sem("tab")

        x_tiles = x.rearrange("b (i p) c -> p (b i) c", p=P)
        NOUT = 2 * 3 * GB + 1
        block = ctx.enter_context(nc.Block())

        @block.sync
        def _(sp):
            def load_x(g):
                lot = slice(g * GT, (g + 1) * GT)
                sp.dma_start(xs[:, lot, :], x_tiles[:, lot, :]).then_inc(x_in[g], 16)

            load_x(0)
            sp.dma_start(w_sb[:, :], w_attn).then_inc(w_in, 16)
            load_x(1)
            sp.dma_start(k127h[:, :], e_k127h).then_inc(vec_in, 16)
            sp.dma_start(v127[:, :], e_v127).then_inc(vec_in, 16)
            load_x(2)
            load_x(3)
            for dst, src in ((ek[:, :], e_k), (k127[:, :], e_k127), (rowsel[:, :], part_of_row),
                             (t["tv"][:, :, :], e_v)):
                sp.dma_start(dst, src).then_inc(tab_in, 16)
            sp.dma_start(t["wp"][:, :, :], w_proj).then_inc(wp_in, 16)
            for g in range(G):
                for n, (dst, third) in enumerate(((q_parts, 0), (k_parts, 1))):
                    sp.wait_ge(p3_done, 2 * g + 1 + n)
                    for m in range(3):
                        for b in range(GB):
                            src = parts[:, g % 2, third, m, b * T:(b + 1) * T]
                            sp.dma_start(dst[m, :, g * GB + b, :, :].rearrange("d h t -> h d t"),
                                         src).then_inc(out_done[g % 2], 16)
                sp.wait_ge(vg_done, g + 1)
                sp.dma_start(v_dram[:, g * GT:(g + 1) * GT, :], vg[:, g % 2, :, :]).then_inc(out_done[g % 2], 16)
            for n in range(2):
                sp.wait_ge(out_done[n], 16 * NOUT * G // 2)
            sp.wait_ge(wp_in, 16)

        @block.gpsimd
        def _(pool):
            nc.gpsimd.memset(t["ident"][:, :], 0.0).then_inc(id_done, 1)
            wait(pool, id_done, 1)
            nc.gpsimd.affine_select(out=t["ident"][:, :], in_=t["ident"][:, :], compare_op=ALU.not_equal, fill=1.0,
                                    base=0, pattern=[[-1, P]], channel_multiplier=1).then_inc(id_done, 1)
            nc.gpsimd.memset(t["kb"][:, :, :], 0.0)
            nc.gpsimd.memset(t["qb"][:, :, :, :], 0.0)
            for g in range(G):
                for n in range(2):
                    wait(pool, p2_done, 2 * g + 1 + n)
                    nc.gpsimd.tensor_tensor(parts[:, g % 2, n, 2, :], rest[:, g % 2, n, :], parts[:, g % 2, n, 1, :],
                                            ALU.subtract).then_inc(p3_done, 1)

        @block.tensor
        def _(pe):
            wait(pe, id_done, 2)
            pe.wait_ge(w_in, 16)
            for g in range(G):
                pe.wait_ge(xn_done, g + 1)
                wait(pe, xnT_done, 2 * g)
                for n in range(GT):
                    ins = nc.tensor.transpose(xT_ps[:, n // 4, (n % 4) * P:(n % 4 + 1) * P], xs[:, g * GT + n, :],
                                              t["ident"][:, :])
                    if n % 4 == 3:
                        ins.then_inc(xT_ready, 1)
                wait(pe, xnT_done, 2 * g + 2)
                wait(pe, rest_done, 2 * g)
                for n in range(2):
                    nc.tensor.matmul(q_ps[:, n, :], w_sb[:, 0:C], xnT[:, g % 2, n * 512:(n + 1) * 512],
                                     start=True, stop=True).then_inc(q_ready, 1)
                for n in range(2):
                    nc.tensor.matmul(k_ps[:, n, :], w_sb[:, C:2 * C], xnT[:, g % 2, n * 512:(n + 1) * 512],
                                     start=True, stop=True).then_inc(k_ready, 1)
                wait(pe, vg_done, g)
                for n in range(GT):
                    ins = nc.tensor.matmul(v_ps[:, n // 4, (n % 4) * P:(n % 4 + 1) * P], xnT[:, g % 2, n * P:(n + 1) * P],
                                           w_sb[:, 2 * C:3 * C], start=True, stop=True)
                ins.then_inc(v_ready, 1)

        @block.scalar
        def _(act):
            def stats(g):
                lot = slice(g * GT, (g + 1) * GT)
                act.wait_ge(xc_done, g + 1)
                wait(act, ssq_done, g)
                nc.scalar.activation(sq[:, :, :], xs[:, lot, :], ACT.Square).then_inc(sq_done, 1)
                act.wait_ge(var_done, g + 1)
                nc.scalar.activation(stat[:, 4, lot], stat[:, 3, lot], ACT.Sqrt).then_inc(sd_done, 1)

            def split(g):
                h = g % 2
                wait(act, v_ready, g - 1)
                for n in range(2):
                    act.wait_ge(xT_ready, 2 * g + 1 + n)
                    nc.scalar.activation(xnT[:, h, n * 512:(n + 1) * 512], xT_ps[:, n, :], ACT.Copy).then_inc(xnT_done, 1)
                wait(act, out_done[h], 16 * NOUT * (g // 2))
                act.wait_ge(q_ready, 2 * g + 2)
                nc.scalar.activation(parts[:, h, 0, 0, :], q_ps[:, :, :], ACT.Copy).then_inc(p1_done, 1)
                act.wait_ge(k_ready, 2 * g + 2)
                act.wait_ge(bias_done, 1)
                nc.scalar.activation(k32[:, h, :], k_ps[:, :, :], ACT.Identity, bias=nk127h[:, 0:1],
                                     scale=-float(SCALE)).then_inc(k32_done, 1)
                act.wait_ge(k32_done, g + 1)
                nc.scalar.activation(parts[:, h, 1, 0, :], k32[:, h, :], ACT.Copy).then_inc(p1_done, 1)
                for n in range(2):
                    act.wait_ge(rest_done, 2 * g + 1 + n)
                    nc.scalar.activation(parts[:, h, n, 1, :], rest[:, h, n, :], ACT.Copy).then_inc(p2_done, 1)

            stats(0)
            for g in range(G):
                if g + 1 < G:
                    stats(g + 1)
                if g:
                    split(g - 1)
            split(G - 1)

        @block.vector
        def _(dve):
            def stats(g):
                lot = slice(g * GT, (g + 1) * GT)
                dve.wait_ge(x_in[g], 16)
                nc.vector.tensor_reduce(stat[:, 0, lot], xs[:, lot, :], AX.X, ALU.add).then_inc(sum_done, 1)
                dve.wait_ge(sum_done, g + 1)
                nc.vector.tensor_scalar(stat[:, 1, lot], stat[:, 0, lot], 1.0 / C, None, ALU.mult).then_inc(mean_done, 1)
                dve.wait_ge(mean_done, g + 1)
                nc.vector.tensor_tensor(xs[:, lot, :], xs[:, lot, :],
                                        stat[:, 1, lot].unsqueeze(2).to_broadcast([P, GT, C]),
                                        ALU.subtract).then_inc(xc_done, 1)
                dve.wait_ge(sq_done, g + 1)
                nc.vector.tensor_reduce(stat[:, 2, lot], sq[:, :, :], AX.X, ALU.add).then_inc(ssq_done, 1)
                dve.wait_ge(ssq_done, g + 1)
                nc.vector.tensor_scalar(stat[:, 3, lot], stat[:, 2, lot], 1.0 / C, EPS, ALU.mult,
                                        ALU.add).then_inc(var_done, 1)
                dve.wait_ge(sd_done, g + 1)
                nc.vector.reciprocal(rstd[:, lot], stat[:, 4, lot]).then_inc(rstd_done, 1)
                dve.wait_ge(rstd_done, g + 1)
                dve.wait_ge(xc_done, g + 1)
                nc.vector.tensor_tensor(xs[:, lot, :], xs[:, lot, :],
                                        rstd[:, lot].unsqueeze(2).to_broadcast([P, GT, C]),
                                        ALU.mult).then_inc(xn_done, 1)

            def split(g):
                h = g % 2
                wait(dve, p3_done, 2 * (g - 1))
                dve.wait_ge(p1_done, 2 * g + 1)
                nc.vector.tensor_tensor(rest[:, h, 0, :], q_ps[:, :, :].rearrange("p a n -> p (a n)"),
                                        parts[:, h, 0, 0, :], ALU.subtract).then_inc(rest_done, 1)
                dve.wait_ge(p1_done, 2 * g + 2)
                nc.vector.tensor_tensor(rest[:, h, 1, :], k32[:, h, :], parts[:, h, 1, 0, :],
                                        ALU.subtract).then_inc(rest_done, 1)
                dve.wait_ge(v_ready, g + 1)
                wait(dve, out_done[h], 16 * NOUT * (g // 2))
                nc.vector.tensor_tensor(vg[:, h, :, :], v_ps[:, :, :].rearrange("p a (n c) -> p (a n) c", c=C),
                                        v127[:, :].unsqueeze(1).to_broadcast([P, GT, C]),
                                        ALU.add).then_inc(vg_done, 1)

            def tables():
                dve.wait_ge(tab_in, 16 * 4)
                nc.vector.memset(t["te"][:, :], 0.0).then_inc(tab, 1)
                dve.wait_ge(vec_in, 16 * 2)
                nc.vector.tensor_scalar(ekr[:, 0, :], ek[:, :], -1.0, k127[:, 0:1], ALU.mult, ALU.add).then_inc(tab, 1)
                dve.wait_ge(tab, 2)
                nc.vector.tensor_tensor(t["tv"][:, :, :], t["tv"][:, :, :],
                                        v127[:, 0:D].unsqueeze(1).to_broadcast([P, NREL, D]), ALU.subtract).then_inc(tab, 1)
                nc.vector.tensor_copy(ekp[:, 0, :], ekr[:, 0, :]).then_inc(tab, 1)
                dve.wait_ge(tab, 4)
                nc.vector.tensor_tensor(ekr[:, 1, :], ekr[:, 0, :], ekp[:, 0, :], ALU.subtract).then_inc(tab, 1)
                dve.wait_ge(tab, 5)
                nc.vector.tensor_copy(ekp[:, 1, :], ekr[:, 1, :]).then_inc(tab, 1)
                dve.wait_ge(tab, 6)
                nc.vector.tensor_tensor(ekp[:, 2, :], ekr[:, 1, :], ekp[:, 1, :], ALU.subtract).then_inc(tab, 1)
                dve.wait_ge(tab, 7)
                nc.vector.tensor_scalar(ekr[:, 0, :], ekp[:, 0, :], rowsel[:, 0:1], None, ALU.mult).then_inc(tab, 1)
                dve.wait_ge(tab, 8)
                nc.vector.scalar_tensor_tensor(out=ekr[:, 1, :], in0=ekp[:, 1, :], scalar=rowsel[:, 1:2],
                                               in1=ekr[:, 0, :], op0=ALU.mult, op1=ALU.add).then_inc(tab, 1)
                dve.wait_ge(tab, 9)
                nc.vector.scalar_tensor_tensor(out=t["te"][0:KR, :], in0=ekp[:, 2, :], scalar=rowsel[:, 2:3],
                                               in1=ekr[:, 1, :], op0=ALU.mult, op1=ALU.add).then_inc(tab, 1)

            dve.wait_ge(vec_in, 16 * 2)
            nc.vector.tensor_scalar(nk127h[:, :], k127h[:, :], -1.0, None, ALU.mult).then_inc(bias_done, 1)
            stats(0)
            for g in range(G):
                if g + 1 < G:
                    stats(g + 1)
                if g:
                    split(g - 1)
            tables()
            split(G - 1)


def attention_part(nc, t, x, q_parts, k_parts, v_dram, x1_dram):
    bank_of, use_before = bank_plan()
    with ExitStack() as ctx:
        sb = lambda name, shape, dt: ctx.enter_context(nc.sbuf_tensor(name, shape, dt))
        ps = lambda name, shape: ctx.enter_context(nc.psum_tensor(name, shape, F32))
        signals = []

        def sem(name):
            signals.append(ctx.enter_context(nc.semaphore(name)))
            return signals[-1]

        ident, te, tv, wp = t["ident"], t["te"], t["tv"], t["wp"]
        kb, qb, vb = t["kb"], t["qb"], t["vb"]
        xr = sb("xr", [P, GB * NI, C], F32)
        relS = sb("relS", [P, 2, P, NH], F32)
        rc = sb("rc", [P, 2, 4, P], F32)
        near = sb("near", [P, 2, 4, NI, P], F32)
        nmin = sb("nmin", [P, NI, NH], F32)
        prob = sb("prob", [P, 6, T], F32)
        pT = sb("pT", [P, 2, 4, T], F32)
        ptmp = sb("ptmp", [P, 4, P], F32)
        pcT = sb("pcT", [P, 2, NH, P], F32)
        rsb = sb("rsb", [P, 32, NH], F32)
        den = sb("den", [P, NI, NH], F32)
        rden = sb("rden", [P, NH], F32)
        rden32 = sb("rden32", [P, NH * 32], F32)
        y = sb("y", [P, GB, T], F32)
        x1 = sb("x1", [P, 2, GB, C], F32)

        qk_ps = ps("qk_ps", [P, 2, 512])
        ring_ps = ps("ring_ps", [P, 4, 512])
        av_ps = ps("av_ps", [P, GB, 512])

        k_in = sem("k_in")
        q_in = [sem(f"q_in{n}") for n in range(2)]
        v_in = sem("v_in")
        xr_in = sem("xr_in")
        rel_ready = sem("rel_ready")
        rel_done = sem("rel_done")
        tr_ready = sem("tr_ready")
        rc_done = sem("rc_done")
        near_done = sem("near_done")
        qk_ready = sem("qk_ready")
        min_done = sem("min_done")
        exp_done = sem("exp_done")
        tp_ready = sem("tp_ready")
        pTa_done = sem("pTa_done")
        pTv_done = sem("pTv_done")
        ptmp_done = sem("ptmp_done")
        pc_done = sem("pc_done")
        av_done = sem("av_done")
        rv_ready = sem("rv_ready")
        rsb_done = sem("rsb_done")
        rt_ready = sem("rt_ready")
        ysum_done = sem("ysum_done")
        av_copied = sem("av_copied")
        rden32_done = sem("rden32_done")
        dn_ready = sem("dn_ready")
        rden_done = sem("rden_done")
        y_done = sem("y_done")
        pj_ready = sem("pj_ready")
        x1_done = sem("x1_done")
        x1_out = [sem(f"x1_out{n}") for n in range(2)]
        clear_done = ctx.enter_context(nc.semaphore("clear_done"))

        def copied(i, n):
            return (pTa_done if on_act(i, n) else pTv_done, copies(on_act(i, n), i, n))

        def wait_copied(engine, i, n):
            wait(engine, pTa_done, copies(True, i, n))
            wait(engine, pTv_done, copies(False, i, n))

        READ = {
            "rel": lambda i, c: (rel_done, 8 * (i - 1) + c + 1),
            "tr": lambda i, u: (rc_done, QUADS * i + u),
            "dn": lambda i, b: (y_done, GB * i + b + 1),
            "pj": lambda i: (x1_done, i + 1),
            "tp": copied,
            "rv": lambda i, c: (rsb_done, RVN * i + c + 1),
            "rt": lambda i, b: (ysum_done, GB * i + b + 1),
        }

        x_tiles = x.rearrange("b (i p) c -> p (b i) c", p=P)
        x1_tiles = x1_dram.rearrange("b (i p) c -> p b i c", p=P)
        cleared = range(min(q.num for q in signals), max(q.num for q in signals) + 1)

        def load_q(sp, group, i):
            for part, m in enumerate(Q_PART):
                src = q_parts[m, :, bass.ds(group * GB, GB), :, i * P:(i + 1) * P]
                sp.dma_start(qb[8 * part:8 * part + 8, i % 2, :, :],
                             src.rearrange("d b h t -> d (b h) t")).then_inc(q_in[i % 2], 16)

        def load_k(sp, group, b):
            for part, m in enumerate(K_PART):
                src = k_parts[m, :, bass.ds(group * GB + b, 1), :, :].rearrange("d a h t -> d (a h) t")
                sp.dma_start(kb[8 * part:8 * part + 8, b * H:(b + 1) * H, :], src).then_inc(k_in, 16)

        def load_v(sp, group):
            sp.dma_start(vb[:, :, :], v_dram[:, bass.ds(group * GB * NI, GB * NI), :]).then_inc(v_in, 16)

        def mask_seen(k):
            return nc.gpsimd.affine_select(out=near[:, k % 2, :, NI - 1, :], in_=rc[:, k % 2, :, :],
                                           compare_op=ALU.is_ge, fill=BIG, base=0, pattern=[[0, 4], [-1, P]],
                                           channel_multiplier=1)

        with nc.Block() as block:

            @block.sync
            def _(sp):
                load_q(sp, 0, 0)
                for b in range(GB):
                    load_k(sp, 0, b)
                load_v(sp, 0)
                sp.wait_ge(k_in, 96 * GB)
                sp.wait_ge(v_in, 16)

            @block.vector
            def _(dve):
                nc.vector.memset(av_ps[:, :, :], 0.0)
                nc.vector.memset(ring_ps[:, :, :], 0.0).then_inc(clear_done, 1)
                nc.vector.memset(near[:, :, :, 0:NI - 2, :], 0.0).then_inc(clear_done, 1)
                dve.wait_ge(clear_done, 2)

            @block.tensor
            def _(pe):
                pe.wait_ge(clear_done, 1)
                pe.wait_ge(q_in[0], 96)
                for c in range(8):
                    wait(pe, rel_done, c - 3)
                    for a in range(16):
                        tau = 16 * c + a
                        ins = nc.tensor.matmul(ring_ps[:, c % 4, a * NH:(a + 1) * NH], te[:, P - tau:2 * P - tau],
                                               qb[:, 0, :, tau], start=True, stop=True)
                    ins.then_inc(rel_ready, 1)
                pe.wait_ge(rel_done, 8)
                for q in range(4):
                    ins = nc.tensor.transpose(ring_ps[:, 0, q * P:(q + 1) * P], relS[:, 0, :, q], ident[:, :])
                ins.then_inc(tr_ready, 1)

            @block.scalar
            def _(act):
                for c in range(8):
                    act.wait_ge(rel_ready, c + 1)
                    nc.scalar.activation(relS[:, 0, 16 * c:16 * (c + 1), :],
                                         ring_ps[:, c % 4, :].rearrange("p (t n) -> p t n", n=NH),
                                         ACT.Copy).then_inc(rel_done, 1)
                act.wait_ge(tr_ready, 1)
                nc.scalar.activation(rc[:, 0, :, :], ring_ps[:, 0, :].rearrange("p (q t) -> p q t", t=P),
                                     ACT.Copy).then_inc(rc_done, 1)

            @block.gpsimd
            def _(pool):
                pool.wait_ge(rc_done, 1)
                mask_seen(0).then_inc(near_done, 1)
                pool.wait_ge(near_done, 1)

        nc.all_engine_barrier(sems_to_clear=cleared)

        with nc.Fori(0, G) as g:
            with nc.Block() as block:

                @block.sync
                def _(sp):
                    def next_q(i):
                        wait(sp, qk_ready, NH * (i - 1))
                        if i < NI:
                            load_q(sp, g, i)
                        else:
                            load_q(sp, (g + 1) % G, 0)

                    def store(i):
                        sp.wait_ge(x1_done, i + 1)
                        sp.dma_start(x1_tiles[:, bass.ds(g * GB, GB), i, :],
                                     x1[:, i % 2, :, :]).then_inc(x1_out[i % 2], 16)

                    next_q(1)
                    sp.dma_start(xr[:, :, :], x_tiles[:, bass.ds(g * GB * NI, GB * NI), :]).then_inc(xr_in, 16)
                    for i in range(2, NI + 1):
                        next_q(i)
                        if i >= 3:
                            store(i - 3)
                    for b in range(GB):
                        sp.wait_ge(qk_ready, HEADS - NH + H * (b + 1))
                        load_k(sp, (g + 1) % G, b)
                    store(NI - 2)
                    sp.wait_ge(av_done, QUADS * NI)
                    load_v(sp, (g + 1) % G)
                    store(NI - 1)
                    sp.wait_ge(k_in, 96 * GB)
                    sp.wait_ge(q_in[0], 96 * 2)
                    sp.wait_ge(v_in, 16)
                    for n in range(2):
                        sp.wait_ge(x1_out[n], 16 * NI // 2)

                @block.gpsimd
                def _(pool):
                    def masks(i, u):
                        k = QUADS * i + u
                        pool.wait_ge(rc_done, k)
                        wait(pool, min_done, 4 * (k - 1))
                        if 0 < i < NI:
                            nc.gpsimd.affine_select(out=near[:, k % 2, :, NI - 2, :], in_=rc[:, k % 2, :, :],
                                                    compare_op=ALU.is_gt, fill=0.0, base=0, pattern=[[0, 4], [1, P]],
                                                    channel_multiplier=-1)
                        mask_seen(k).then_inc(near_done, 1)

                    def near_probs(i, u):
                        k = QUADS * (i - 1) + u
                        wait_copied(pool, i, 4 * u + 3)
                        wait(pool, pc_done, k)
                        nc.gpsimd.affine_select(out=ptmp[:, :, :], in_=pT[:, u % 2, :, (i - 1) * P:i * P],
                                                compare_op=ALU.is_gt, fill=0.0, base=0, pattern=[[0, 4], [-1, P]],
                                                channel_multiplier=1).then_inc(ptmp_done, 1)
                        pool.wait_ge(ptmp_done, k + 1)
                        if u == 0:
                            wait(pool, rv_ready, RVN * (i - 1))
                        nc.gpsimd.tensor_tensor(pcT[:, i % 2, 4 * u:4 * u + 4, :], ptmp[:, :, :],
                                                pT[:, u % 2, :, i * P:(i + 1) * P], ALU.add).then_inc(pc_done, 1)

                    for s in range(SLOTS):
                        if s % 4 == 2 and s + 2 <= HEADS:
                            masks(*divmod((s + 2) // 4, QUADS))
                        if s % 4 == 1 and NH <= s - 9 < HEADS:
                            near_probs(*divmod((s - 9) // 4, QUADS))

                @block.tensor
                def _(pe):
                    def take(*use):
                        if use in use_before:
                            kind, *what = use_before[use]
                            pe.wait_ge(*READ[kind](*what))
                        return ring_ps[:, bank_of[use], :]

                    def rel(i, c):
                        if c == 0:
                            pe.wait_ge(q_in[i % 2], 96 * ((i + 1) // 2))
                        bank = take("rel", i, c)
                        for a in range(16):
                            tau = 16 * c + a
                            ins = nc.tensor.matmul(bank[:, a * NH:(a + 1) * NH], te[:, P - tau:2 * P - tau],
                                                   qb[:, i % 2, :, tau], start=True, stop=True)
                        ins.then_inc(rel_ready, 1)

                    def tr(i, u):
                        if u == 0:
                            pe.wait_ge(rel_done, 8 * i)
                        bank = take("tr", i, u)
                        for q in range(4):
                            ins = nc.tensor.transpose(bank[:, q * P:(q + 1) * P], relS[:, i % 2, :, 4 * u + q], ident[:, :])
                        ins.then_inc(tr_ready, 1)

                    def qk(i, n):
                        k = NH * i + n
                        wait(pe, exp_done, k - 1)
                        nc.tensor.matmul(qk_ps[:, k % 2, 0:(i + 1) * P], qb[:, i % 2, n, :], kb[:, n, 0:(i + 1) * P],
                                         start=True, stop=True).then_inc(qk_ready, 1)

                    def tp(i, n):
                        k = NH * i + n
                        bank = take("tp", i, n)
                        pe.wait_ge(exp_done, k + 1)
                        for j in range(i + 1):
                            ins = nc.tensor.transpose(bank[:, j * P:(j + 1) * P],
                                                      prob[:, k % 6, j * P:(j + 1) * P], ident[:, :])
                        ins.then_inc(tp_ready, 1)

                    def av(i, u):
                        b, hq = divmod(4 * u, H)
                        if i and hq == 0:
                            pe.wait_ge(av_copied, GB * (i - 1) + b + 1)
                        wait_copied(pe, i, 4 * u + 3)
                        for j in range(i + 1):
                            for q in range(4):
                                rhs = pT[:, u % 2, q, j * P:(j + 1) * P] if i else pcT[:, 0, 4 * u + q, :]
                                ins = nc.tensor.matmul(av_ps[32 * q:32 * q + D, b, hq // 4 * P:(hq // 4 + 1) * P],
                                                       vb[:, b * NI + j, (hq + q) * D:(hq + q + 1) * D], rhs,
                                                       start=(hq == 0 and j == 0), stop=(hq + 4 == H and j == i),
                                                       skip_group_check=True)
                        ins.then_inc(av_done, 1)

                    def rv(i, c):
                        if c == 0:
                            if i:
                                pe.wait_ge(pc_done, QUADS * i)
                            else:
                                wait_copied(pe, 0, NH - 1)
                        bank = take("rv", i, c)
                        for a in range(32 // RVN):
                            for tq in range(4):
                                tau = 32 * tq + 32 // RVN * c + a
                                ins = nc.tensor.matmul(bank[32 * tq:32 * tq + D, a * NH:(a + 1) * NH], tv[:, tau, :],
                                                       pcT[:, i % 2, :, tau], start=True, stop=True)
                        ins.then_inc(rv_ready, 1)

                    def rt(i, b):
                        if b == 0:
                            pe.wait_ge(rsb_done, RVN * (i + 1))
                        bank = take("rt", i, b)
                        for tq in range(4):
                            for q in range(4):
                                dst = bank[32 * q:32 * q + D, :].rearrange("d (u t) -> d u t", t=P)
                                ins = nc.tensor.matmul(
                                    dst[:, :, 32 * tq:32 * tq + 32], ident[:, 32 * tq:32 * tq + D],
                                    rsb[:, :, H * b + q:H * (b + 1):4].rearrange("p t u -> p u t"),
                                    start=True, stop=True)
                        ins.then_inc(rt_ready, 1)

                    def dn(i, b):
                        pe.wait_ge(rden32_done, i + 1)
                        bank = take("dn", i, b)
                        for u in range(4):
                            h = b * H + 4 * u
                            ins = nc.tensor.matmul(bank[:, u * P:(u + 1) * P], rden32[:, 32 * h:32 * (h + 4)],
                                                   ident[:, :], start=True, stop=True)
                        ins.then_inc(dn_ready, 1)

                    def pj(i):
                        pe.wait_ge(y_done, GB * (i + 1))
                        bank = take("pj", i)
                        for b in range(GB):
                            for u in range(4):
                                ins = nc.tensor.matmul(bank[:, b * C:(b + 1) * C], y[:, b, u * P:(u + 1) * P],
                                                       wp[:, u, :], start=(u == 0), stop=(u == 3))
                        ins.then_inc(pj_ready, 1)

                    do = {"rel": rel, "tr": tr, "qk": qk, "tp": tp, "av": av, "rv": rv, "rt": rt, "dn": dn, "pj": pj}
                    for s in range(SLOTS):
                        for kind, *what in pe_slot(s):
                            do[kind](*what)

                @block.scalar
                def _(act):
                    def rel_copy(i, c):
                        act.wait_ge(rel_ready, 8 * (i - 1) + c + 1)
                        if c == 0:
                            wait(act, tr_ready, QUADS * (i - 1) - 1)
                        bank = ring_ps[:, bank_of["rel", i, c], :]
                        nc.scalar.activation(relS[:, i % 2, 16 * c:16 * (c + 1), :],
                                             bank.rearrange("p (t n) -> p t n", n=NH),
                                             ACT.Copy).then_inc(rel_done, 1)

                    def rc_copy(i, u):
                        k = QUADS * i + u
                        act.wait_ge(tr_ready, k)
                        wait(act, near_done, k - 2)
                        nc.scalar.activation(rc[:, k % 2, :, :],
                                             ring_ps[:, bank_of["tr", i, u], :].rearrange("p (q t) -> p q t", t=P), ACT.Copy).then_inc(rc_done, 1)

                    def exp(i, n):
                        k = NH * i + n
                        wait(act, tp_ready, k - 5)
                        act.wait_ge(min_done, k + 1)
                        nc.scalar.activation(prob[:, k % 6, 0:(i + 1) * P], qk_ps[:, k % 2, 0:(i + 1) * P],
                                             ACT.Exp, bias=nmin[:, i, n:n + 1], scale=-1.0,
                                             accum_out=den[:, i, n:n + 1]).then_inc(exp_done, 1)

                    def pT_copy(i, n):
                        act.wait_ge(tp_ready, NH * i + n + 1)
                        if i:
                            wait(act, av_done, QUADS * i + n // 4 - 1)
                            wait(act, pc_done, QUADS * (i - 1) + n // 4 - 1)
                        dst = pT[:, n // 4 % 2, n % 4, 0:(i + 1) * P] if i else pcT[:, 0, n, :]
                        nc.scalar.activation(dst, ring_ps[:, bank_of["tp", i, n], 0:(i + 1) * P],
                                             ACT.Copy).then_inc(pTa_done, 1)

                    def rsb_copy(i, c):
                        act.wait_ge(rv_ready, RVN * i + c + 1)
                        if c == 0:
                            wait(act, rt_ready, GB * i)
                        lot = 32 // RVN
                        nc.scalar.activation(rsb[:, lot * c:lot * (c + 1), :],
                                             ring_ps[:, bank_of["rv", i, c], 0:lot * NH].rearrange("p (t n) -> p t n", n=NH),
                                             ACT.Copy).then_inc(rsb_done, 1)

                    def av_copy(i, b):
                        act.wait_ge(av_done, QUADS * i + QUADS // GB * (b + 1))
                        wait(act, pj_ready, i)
                        nc.scalar.activation(y[:, b, :], av_ps[:, b, :], ACT.Copy).then_inc(av_copied, 1)

                    for s in range(SLOTS):
                        for kind, *what in pe_slot(s - 1) if s else []:
                            if kind == "rel":
                                rel_copy(*what)
                            if kind == "tr":
                                rc_copy(*what)
                            if kind == "rv":
                                rsb_copy(*what)
                        if s % NH in (1, 8) and s > NH:
                            av_copy(s // NH - 1, 0 if s % NH == 1 else 1)
                        if 0 <= s - 5 < HEADS and on_act(*divmod(s - 5, NH)):
                            pT_copy(*divmod(s - 5, NH))
                        if s < HEADS:
                            exp(*divmod(s, NH))

                @block.vector
                def _(dve):
                    def scores_min(i, n):
                        k = NH * i + n
                        dve.wait_ge(qk_ready, k + 1)
                        if n % 4 == 0 and k:
                            dve.wait_ge(near_done, k // 4)
                        nb = near[:, k // 4 % 2, n % 4, NI - 1 - i:NI, :]
                        nc.vector.tensor_tensor_reduce(out=qk_ps[:, k % 2, 0:(i + 1) * P],
                                                       in0=qk_ps[:, k % 2, 0:(i + 1) * P],
                                                       in1=nb.rearrange("p a b -> p (a b)"), scale=1.0, scalar=3e38,
                                                       op0=ALU.add, op1=ALU.min,
                                                       accum_out=nmin[:, i, n:n + 1]).then_inc(min_done, 1)

                    def pT_copy(i, n):
                        dve.wait_ge(tp_ready, NH * i + n + 1)
                        if i and n % 4 == 0:
                            wait(dve, av_done, QUADS * i + n // 4 - 1)
                            wait(dve, pc_done, QUADS * (i - 1) + n // 4 - 1)
                        nc.vector.tensor_copy(pT[:, n // 4 % 2, n % 4, 0:(i + 1) * P] if i else pcT[:, 0, n, :],
                                              ring_ps[:, bank_of["tp", i, n], 0:(i + 1) * P]).then_inc(pTv_done, 1)

                    def invert(i):
                        dve.wait_ge(exp_done, NH * (i + 1))
                        nc.vector.reciprocal(rden[:, :], den[:, i, :]).then_inc(rden_done, 1)
                        wait(dve, dn_ready, GB * i)
                        dve.wait_ge(rden_done, i + 1)
                        nc.vector.tensor_copy(rden32[:, :].rearrange("p (h r) -> p h r", r=32),
                                              rden[:, :].unsqueeze(2).to_broadcast([P, NH, 32])).then_inc(rden32_done, 1)

                    def add_relative(i, b):
                        dve.wait_ge(av_copied, GB * i + b + 1)
                        dve.wait_ge(rt_ready, GB * i + b + 1)
                        nc.vector.tensor_tensor(y[:, b, :], y[:, b, :], ring_ps[:, bank_of["rt", i, b], :],
                                                ALU.add).then_inc(ysum_done, 1)

                    def normalise(i, b):
                        dve.wait_ge(dn_ready, GB * i + b + 1)
                        dve.wait_ge(ysum_done, GB * i + b + 1)
                        nc.vector.tensor_tensor(y[:, b, :], y[:, b, :], ring_ps[:, bank_of["dn", i, b], :],
                                                ALU.mult).then_inc(y_done, 1)

                    def residual(i):
                        if i == 0:
                            dve.wait_ge(xr_in, 16)
                        dve.wait_ge(pj_ready, i + 1)
                        wait(dve, x1_out[i % 2], 16 * (i // 2))
                        nc.vector.tensor_tensor(x1[:, i % 2, :, :],
                                                ring_ps[:, bank_of["pj", i], 0:GB * C].rearrange("p (b c) -> p b c", b=GB),
                                                xr[:, :, :].rearrange("p (b i) c -> p b i c", b=GB)[:, :, i, :],
                                                ALU.add).then_inc(x1_done, 1)

                    for s in range(SLOTS):
                        if 0 <= s - 5 < HEADS and not on_act(*divmod(s - 5, NH)):
                            pT_copy(*divmod(s - 5, NH))
                        if s < HEADS:
                            scores_min(*divmod(s, NH))
                        if s % NH == 0 and s:
                            invert(s // NH - 1)
                        for kind, *what in pe_slot(s - 1) if s else []:
                            if kind == "rt":
                                add_relative(*what)
                            if kind == "dn":
                                normalise(*what)
                            if kind == "pj":
                                residual(*what)

            nc.all_engine_barrier(sems_to_clear=cleared)


def expert_part(nc, t, x1_dram, gate_w, gate_bias, w1, w3, w2, out):
    NM = NSH + E
    with ExitStack() as ctx:
        sb = lambda name, shape, dt: ctx.enter_context(nc.sbuf_tensor(name, shape, dt))
        signals = []

        def sem(name):
            signals.append(ctx.enter_context(nc.semaphore(name)))
            return signals[-1]

        ps = lambda name, shape: ctx.enter_context(nc.psum_tensor(name, shape, F32))
        CT = CH // P
        NG = 4
        LT = TILES // NG
        TURNS = 2
        CHUNKS = TILES // CT // TURNS
        NU = E + 1
        AC = 1 + CT * E
        w1_sb = sb("w1_sb", [P, NM, P], F32)
        w3_sb = sb("w3_sb", [P, NM, P], F32)
        w2_sb = sb("w2_sb", [P, NM, P], F32)
        gw = sb("gw", [P, E], F32)
        gb = sb("gb", [P, E], F32)
        x1s = sb("x1s", [P, TILES, C], F32)
        xc = sb("xc2", [P, TILES, C], F32)
        sq = sb("sq2", [P, 4, C], F32)
        stat = sb("stat2", [P, 5, TILES], F32)
        rstd = sb("rstd2", [P, TILES], F32)
        rch = sb("rch", [P, 2, CT], F32)
        xn = sb("xn2", [P, 2, CT, C], F32)
        xnT = sb("xnT2", [P, 2, CH], F32)
        gates = sb("gates", [P, 2, CT, E], F32)
        order = sb("order", [P, E], F32)
        lg = sb("lg", [P, CT, E], F32)
        score = sb("score", [P, CT, E], F32)
        biased = sb("biased", [P, CT, E], F32)
        pick = sb("pick", [P, 2, CT, E], F32)
        tmp = sb("tmp", [P, CT, E], F32)
        red = sb("red", [P, 3 + 2 * TOPK, CT], F32)
        silu = sb("silu", [P, 2, CH], F32)
        hT = sb("hT", [P, 4, CH], F32)
        acc = sb("acc", [P, 2, CT, C], F32)
        h1_ps = ps("h1_ps", [P, 2, 512])
        h3_ps = ps("h3_ps", [P, 2, 512])
        y_ps = ps("y_ps", [P, 2, 512])
        xT_ps = ps("xT2_ps", [P, 512])
        lg_ps = ps("lg_ps", [P, 512])

        w_in = ctx.enter_context(nc.semaphore("w2_in"))
        x1_in = [ctx.enter_context(nc.semaphore(f"x1_in{n}")) for n in range(NG)]
        order_done = ctx.enter_context(nc.semaphore("order_done"))
        sum_done = ctx.enter_context(nc.semaphore("sum2_done"))
        mean_done = ctx.enter_context(nc.semaphore("mean2_done"))
        xc_done = ctx.enter_context(nc.semaphore("xc2_done"))
        ssq_done = ctx.enter_context(nc.semaphore("ssq2_done"))
        var_done = ctx.enter_context(nc.semaphore("var2_done"))
        sd_done = ctx.enter_context(nc.semaphore("sd2_done"))
        rstd_done = ctx.enter_context(nc.semaphore("rstd2_done"))
        rch_done = sem("rch_done")
        xn_done = sem("xn2_done")
        xT_ready = sem("xT2_ready")
        xnT_done = sem("xnT2_done")
        lg_ready = sem("lg_ready")
        sh_done = sem("sh_done")
        ex_done = sem("ex_done")
        gates_done = sem("gates_done")
        chain = sem("chain2")
        h1_ready = sem("h1_ready")
        h3_ready = sem("h3_ready")
        silu_done = sem("silu_done")
        hT_done = sem("hT_done")
        y_ready = sem("y_ready")
        acc_done = sem("acc_done")
        out_done = [sem(f"out_done2{n}") for n in range(2)]
        cleared = range(min(q.num for q in signals), max(q.num for q in signals) + 1)

        def additions(k):
            return AC * (k // NU) + 1 + CT * (k % NU) if k >= 0 else 0


        def held(c):
            return (c - 1) % 2

        def scales(dve, at, j, buf):
            wait(dve, xn_done, j - 1)
            nc.vector.tensor_copy(rch[:, buf, :], rstd[:, bass.ds(at, CT)]).then_inc(rch_done, 1)

        def normalise(act, at, j, buf):
            act.wait_ge(rch_done, j + 1)
            wait(act, xT_ready, j - 1)
            for n in range(CT):
                ins = nc.scalar.activation(xn[:, buf, n:n + 1, :], xc[:, bass.ds(at + n, 1), :], ACT.Copy,
                                           scale=rch[:, buf, n:n + 1])
            ins.then_inc(xn_done, 1)

        def turn_tiles(pe, j, buf):
            pe.wait_ge(xn_done, j + 1)
            wait(pe, xnT_done, j)
            for n in range(CT):
                ins = nc.tensor.transpose(xT_ps[:, n * P:(n + 1) * P], xn[:, buf, n, :], t["ident"][:, :])
            ins.then_inc(xT_ready, 1)

        def copy_turned(act, j, buf):
            act.wait_ge(xT_ready, j + 1)
            nc.scalar.activation(xnT[:, buf, :], xT_ps[:, :], ACT.Copy).then_inc(xnT_done, 1)

        def gate_scores(pe, j, buf):
            pe.wait_ge(xnT_done, j + 1)
            wait(pe, sh_done, j)
            for n in range(CT):
                ins = nc.tensor.matmul(lg_ps[:, n * E:(n + 1) * E], xnT[:, buf, n * P:(n + 1) * P], gw[:, :],
                                       start=True, stop=True)
            ins.then_inc(lg_ready, 1)

        def exponentials(act, j):
            act.wait_ge(sh_done, j + 1)
            nc.scalar.activation(score[:, :, :], lg[:, :, :], ACT.Exp).then_inc(ex_done, 1)

        NCHAIN = 2 + 3 + 5 * TOPK + TOPK - 1 + 1
        wide = lambda r: red[:, r, :].unsqueeze(2).to_broadcast([P, CT, E])
        rows = lambda v: v[:, :].unsqueeze(1).to_broadcast([P, CT, E])

        def chained(dve, j, first):
            step = [NCHAIN * j + first]

            def then(ins):
                step[0] += 1
                ins.then_inc(chain, 1)
                dve.wait_ge(chain, step[0])
            return then

        def gates_shift(dve, j):
            then = chained(dve, j, 0)
            lgp = lg_ps[:, 0:CT * E].rearrange("p (n e) -> p n e", e=E)
            dve.wait_ge(lg_ready, j + 1)
            then(nc.vector.tensor_reduce(red[:, 0, :], lgp, AX.X, ALU.max))
            nc.vector.tensor_tensor(lg[:, :, :], lgp, wide(0), ALU.subtract).then_inc(sh_done, 1)

        def gates_softmax(dve, j):
            then = chained(dve, j, 1)
            dve.wait_ge(ex_done, j + 1)
            then(nc.vector.tensor_reduce(red[:, 1, :], score[:, :, :], AX.X, ALU.add))
            then(nc.vector.reciprocal(red[:, 2, :], red[:, 1, :]))
            then(nc.vector.tensor_tensor(score[:, :, :], score[:, :, :], wide(2), ALU.mult))
            then(nc.vector.tensor_tensor(biased[:, :, :], score[:, :, :], rows(gb), ALU.add))

        def gates_pick(dve, j, r):
            then = chained(dve, j, 5 + 6 * r)
            then(nc.vector.tensor_reduce(red[:, 3 + 2 * r, :], biased[:, :, :], AX.X, ALU.max))
            then(nc.vector.tensor_tensor(tmp[:, :, :], biased[:, :, :], wide(3 + 2 * r), ALU.is_equal))
            then(nc.vector.tensor_tensor(tmp[:, :, :], tmp[:, :, :], rows(order), ALU.mult))
            then(nc.vector.tensor_reduce(red[:, 4 + 2 * r, :], tmp[:, :, :], AX.X, ALU.max))
            then(nc.vector.tensor_tensor(pick[:, r, :, :], tmp[:, :, :], wide(4 + 2 * r), ALU.is_equal))
            if r + 1 < TOPK:
                then(nc.vector.scalar_tensor_tensor(out=biased[:, :, :], in0=pick[:, r, :, :], scalar=-BIG,
                                                    in1=biased[:, :, :], op0=ALU.mult, op1=ALU.add))

        def gates_write(dve, j, buf):
            then = chained(dve, j, NCHAIN - 1)
            then(nc.vector.tensor_tensor(tmp[:, :, :], pick[:, 0, :, :], pick[:, 1, :, :], ALU.add))
            wait(dve, acc_done, AC * j)
            nc.vector.tensor_tensor(gates[:, buf, :, :], score[:, :, :], tmp[:, :, :],
                                    ALU.mult).then_inc(gates_done, 1)

        x1_tiles = x1_dram.rearrange("b (i p) c -> p (b i) c", p=P)
        out_tiles = out.rearrange("b (i p) c -> p (b i) c", p=P)

        with nc.Block() as block:

            @block.sync
            def _(sp):
                for n in range(NG):
                    lot = slice(n * LT, (n + 1) * LT)
                    sp.dma_start(x1s[:, lot, :], x1_tiles[:, lot, :]).then_inc(x1_in[n], 16)
                for dst, src in ((gw[:, :], gate_w), (gb[:, :], gate_bias), (w1_sb[:, :, :], w1), (w3_sb[:, :, :], w3),
                                 (w2_sb[:, :, :], w2)):
                    sp.dma_start(dst, src).then_inc(w_in, 16)

            @block.gpsimd
            def _(pool):
                for e in range(E):
                    ins = nc.gpsimd.memset(order[:, e:e + 1], float(E - e))
                ins.then_inc(order_done, 1)

            @block.tensor
            def _(pe):
                turn_tiles(pe, 0, held(0))
                pe.wait_ge(w_in, 16 * 5)
                gate_scores(pe, 0, held(0))

            @block.scalar
            def _(act):
                for n in range(TILES):
                    act.wait_ge(xc_done, n // LT + 1)
                    wait(act, ssq_done, n - 3)
                    nc.scalar.activation(sq[:, n % 4, :], xc[:, n, :], ACT.Square,
                                         accum_out=stat[:, 2, n:n + 1]).then_inc(ssq_done, 1)
                act.wait_ge(var_done, 1)
                nc.scalar.activation(stat[:, 4, :], stat[:, 3, :], ACT.Sqrt).then_inc(sd_done, 1)
                normalise(act, 0, 0, held(0))
                copy_turned(act, 0, held(0))
                exponentials(act, 0)

            @block.vector
            def _(dve):
                for n in range(NG):
                    lot = slice(n * LT, (n + 1) * LT)
                    dve.wait_ge(x1_in[n], 16)
                    nc.vector.tensor_reduce(stat[:, 0, lot], x1s[:, lot, :], AX.X, ALU.add).then_inc(sum_done, 1)
                    dve.wait_ge(sum_done, n + 1)
                    nc.vector.tensor_scalar(stat[:, 1, lot], stat[:, 0, lot], 1.0 / C, None, ALU.mult).then_inc(mean_done, 1)
                    dve.wait_ge(mean_done, n + 1)
                    nc.vector.tensor_tensor(xc[:, lot, :], x1s[:, lot, :],
                                            stat[:, 1, lot].unsqueeze(2).to_broadcast([P, LT, C]),
                                            ALU.subtract).then_inc(xc_done, 1)
                dve.wait_ge(ssq_done, TILES)
                nc.vector.tensor_scalar(stat[:, 3, :], stat[:, 2, :], 1.0 / C, EPS, ALU.mult, ALU.add).then_inc(var_done, 1)
                dve.wait_ge(sd_done, 1)
                nc.vector.reciprocal(rstd[:, :], stat[:, 4, :]).then_inc(rstd_done, 1)
                dve.wait_ge(rstd_done, 1)
                scales(dve, 0, 0, held(0))
                dve.wait_ge(w_in, 16 * 5)
                dve.wait_ge(order_done, 1)
                gates_shift(dve, 0)
                gates_softmax(dve, 0)
                for r in range(TOPK):
                    gates_pick(dve, 0, r)
                gates_write(dve, 0, held(0))
                dve.wait_ge(gates_done, 1)

        nc.all_engine_barrier(sems_to_clear=cleared)

        with nc.Fori(0, TURNS) as g:

            def following(c):
                return (g * CHUNKS + c + 1) * CT if c + 1 < CHUNKS else ((g + 1) % TURNS) * CHUNKS * CT

            with nc.Block() as block:

                @block.sync
                def _(sp):
                    for c in range(CHUNKS):
                        sp.wait_ge(acc_done, (c + 1) * AC)
                        sp.dma_start(out_tiles[:, bass.ds((g * CHUNKS + c) * CT, CT), :],
                                     acc[:, c % 2, :, :]).then_inc(out_done[c % 2], 16)
                    for c in range(2):
                        sp.wait_ge(out_done[c], 16 * CHUNKS // 2)

                @block.tensor
                def _(pe):
                    def hidden(c, m):
                        k = NM * c + m
                        rhs = xnT[:, held(c), :]
                        if m == 0:
                            wait(pe, xnT_done, c)
                        wait(pe, silu_done, k - 1)
                        wait(pe, hT_done, k - 1)
                        nc.tensor.matmul(h1_ps[:, k % 2, :], w1_sb[:, m, :], rhs, start=True,
                                         stop=True).then_inc(h1_ready, 1)
                        nc.tensor.matmul(h3_ps[:, k % 2, :], w3_sb[:, m, :], rhs, start=True,
                                         stop=True).then_inc(h3_ready, 1)

                    def product(c, u):
                        k = NU * c + u
                        ms = (0, 1) if u == 0 else (u + 1,)
                        pe.wait_ge(hT_done, NM * c + ms[-1] + 1)
                        wait(pe, acc_done, additions(k - 2))
                        for n in range(CT):
                            for m in ms:
                                ins = nc.tensor.matmul(y_ps[:, k % 2, n * P:(n + 1) * P],
                                                       hT[:, (NM * c + m) % 4, n * P:(n + 1) * P], w2_sb[:, m, :],
                                                       start=(m == ms[0]), stop=(m == ms[-1]))
                        ins.then_inc(y_ready, 1)

                    for c in range(CHUNKS):
                        for m in range(NM):
                            hidden(c, m)
                            if m == 0 and c:
                                product(c - 1, NU - 1)
                            if m >= 2:
                                product(c, m - 2)
                            if m == 2:
                                turn_tiles(pe, c, c % 2)
                            if m == 4:
                                gate_scores(pe, c, c % 2)
                    product(CHUNKS - 1, NU - 1)

                @block.scalar
                def _(act):
                    for c in range(CHUNKS):
                        for m in range(NM):
                            k = NM * c + m
                            act.wait_ge(h1_ready, k + 1)
                            wait(act, hT_done, k - 1)
                            nc.scalar.activation(silu[:, k % 2, :], h1_ps[:, k % 2, :], ACT.Silu).then_inc(silu_done, 1)
                            if m == 1:
                                normalise(act, following(c), c, c % 2)
                            if m == 3:
                                wait(act, h3_ready, NM * c)
                                wait(act, lg_ready, c)
                                copy_turned(act, c, c % 2)
                            if m == 6:
                                exponentials(act, c)

                @block.vector
                def _(dve):
                    def hidden(c, m):
                        k = NM * c + m
                        dve.wait_ge(silu_done, k + 1)
                        dve.wait_ge(h3_ready, k + 1)
                        if k >= 4:
                            cb, mb = divmod(k - 4, NM)
                            dve.wait_ge(y_ready, NU * cb + max(mb - 1, 0) + 1)
                        nc.vector.tensor_tensor(hT[:, k % 4, :], silu[:, k % 2, :], h3_ps[:, k % 2, :],
                                                ALU.mult).then_inc(hT_done, 1)

                    def add(c, u):
                        k = NU * c + u
                        dve.wait_ge(y_ready, k + 1)
                        if u == 0:
                            wait(dve, out_done[c % 2], 16 * (c // 2))
                            ys = y_ps[:, k % 2, :].rearrange("p (n c) -> p n c", c=C)
                            nc.vector.tensor_tensor(acc[:, c % 2, :, :], ys,
                                                    x1s[:, bass.ds((g * CHUNKS + c) * CT, CT), :],
                                                    ALU.add).then_inc(acc_done, 1)
                            return
                        wait(dve, gates_done, c)
                        for n in range(CT):
                            dve.wait_ge(acc_done, AC * c + 1 + (CT * (u - 2) + n + 1 if u > 1 else 0))
                            nc.vector.scalar_tensor_tensor(out=acc[:, c % 2, n, :],
                                                           in0=y_ps[:, k % 2, n * P:(n + 1) * P],
                                                           scalar=gates[:, held(c), n, u - 1:u], in1=acc[:, c % 2, n, :],
                                                           op0=ALU.mult, op1=ALU.add).then_inc(acc_done, 1)

                    for c in range(CHUNKS):
                        for m in range(NM):
                            if m == 0:
                                scales(dve, following(c), c, c % 2)
                            hidden(c, m)
                            if m == 0 and c:
                                add(c - 1, NU - 1)
                            if m >= 2:
                                add(c, m - 2)
                            if m == 5:
                                gates_shift(dve, c)
                            if m == 7:
                                gates_softmax(dve, c)
                            if m in (8, 9):
                                gates_pick(dve, c, m - 8)
                            if m == 9:
                                gates_write(dve, c, c % 2)
                    add(CHUNKS - 1, NU - 1)

            nc.all_engine_barrier(sems_to_clear=cleared)


def block_kernel(nc, x, w_attn, w_proj, e_k, e_k127, e_k127h, e_v, e_v127, part_of_row, gate_w, gate_bias, w1, w3, w2,
                 out):
    q_parts = nc.dram_tensor("q_parts", [3, D, B, H, T], BF16, kind="Internal").ap()
    k_parts = nc.dram_tensor("k_parts", [3, D, B, H, T], BF16, kind="Internal").ap()
    v_dram = nc.dram_tensor("v_dram", [P, TILES, C], F32, kind="Internal").ap()
    x1_dram = nc.dram_tensor("x1_dram", [B, T, C], F32, kind="Internal").ap()
    with ExitStack() as ctx:
        sb = lambda name, shape, dt: ctx.enter_context(nc.sbuf_tensor(name, shape, dt))
        t = {"ident": sb("ident", [P, P], F32),
             "te": sb("te", [P, 2 * NREL], BF16),
             "tv": sb("tv", [P, NREL, D], F32),
             "wp": sb("wp", [P, 4, C], F32),
             "kb": sb("kb", [P, NH, T], BF16),
             "qb": sb("qb", [P, 2, NH, P], BF16),
             "vb": sb("vb", [P, GB * NI, C], F32)}
        qkv_part(nc, t, x, w_attn, w_proj, e_k, e_k127, e_k127h, e_v, e_v127, part_of_row, q_parts, k_parts, v_dram)
        attention_part(nc, t, x, q_parts, k_parts, v_dram, x1_dram)
        expert_part(nc, t, x1_dram, gate_w, gate_bias, w1, w3, w2, out)


def kernel(**inputs):
    import concourse.bacc as bacc
    from concourse.bass_utils import run_bass_kernel_spmd

    a = {k[3:]: np.asarray(v) for k, v in inputs.items()}
    x, ek, ev = a["attn_x"], a["attn_embk"], a["attn_embv"]
    around = (-np.arange(2 * NREL)) % NREL
    turn = (np.arange(NREL)[None, :] - np.arange(P)[:, None]) % NREL
    hidden = lambda shared, experts: np.concatenate([shared.reshape(NSH, P, C), experts]).transpose(2, 0, 1)
    w_proj = np.zeros((4, 32, 4, C), np.float32)
    w_proj[:, :D] = a["attn_w_proj"].reshape(4, 4, D, C).transpose(1, 2, 0, 3)
    arrays = {
        "x": x,
        "w_attn": a["attn_w_attn"],
        "w_proj": w_proj.reshape(P, 4, C),
        "e_k": np.tile(ek[around].T, (len(K_PART), 1)),
        "e_k127": np.tile(ek[-1], len(K_PART))[:, None],
        "e_k127h": np.tile(ek[-1], H)[:, None],
        "e_v": ev[turn],
        "e_v127": np.broadcast_to(np.tile(ev[-1], H), (P, C)),
        "part_of_row": np.repeat(np.eye(3, dtype=np.float32)[K_PART], D, axis=0),
        "gate_w": a["ffn_gate_w"].T,
        "gate_bias": np.broadcast_to(a["ffn_gate_bias"], (P, E)),
        "w1": hidden(a["ffn_sw1"], a["ffn_w1"]),
        "w3": hidden(a["ffn_sw3"], a["ffn_w3"]),
        "w2": np.concatenate([a["ffn_sw2"].T.reshape(NSH, P, C), a["ffn_w2"].transpose(0, 2, 1)]).transpose(1, 0, 2),
    }
    nc = bacc.Bacc("TRN2", target_bir_lowering=False, num_devices=1)
    feed, args = {}, []
    for name, v in arrays.items():
        v = np.ascontiguousarray(v)
        feed[f"in_{name}"] = v
        args.append(nc.dram_tensor(f"in_{name}", v.shape, mybir.dt.from_np(v.dtype), kind="ExternalInput").ap())
    args.append(nc.dram_tensor("out_0", x.shape, F32, kind="ExternalOutput").ap())
    block_kernel(nc, *args)
    r = run_bass_kernel_spmd(nc, [feed], core_ids=[0])
    return r.results[0]["out_0"]
```
